# Optimizing a Trainium2 kernel written in Bass

```python
import numpy as np
import jax
import jax.numpy as jnp

def _softmax(x, axis=-1):
    return jax.nn.softmax(x, axis=axis)

def _gelu(x):
    return jax.nn.gelu(x, approximate=True)

def _silu(x):
    return jax.nn.silu(x)

def _sigmoid(x):
    return jax.nn.sigmoid(x)

def _layernorm(x, axis=-1, eps=1e-05):
    m = jnp.mean(x, axis=axis, keepdims=True)
    v = jnp.var(x, axis=axis, keepdims=True)
    return (x - m) / jnp.sqrt(v + eps)

def _scatter_add(tgt, idx, src, axis=0):
    return tgt.at[idx].add(src)

def _segment_sum(src, seg, n):
    return jax.ops.segment_sum(src, seg, n)
kernel_name = 'mk_xattn_ffn_d4_seqx_r8_2a48ef'

def setup_inputs(seed: int=0):
    np.random.seed(seed)
    _w = jnp.asarray

    def _rec_inputs():
        import jax
        import jax.numpy as jnp
        _rk = jax.random.key(seed)
        x = 7.22e-05 + 1 * jax.random.normal(jax.random.fold_in(_rk, 1), (4, 512, 128), jnp.float32)
        _lenS = 512 - jax.random.randint(jax.random.fold_in(_rk, 7), (4,), 0, max(1, 512 // 4) + 1, jnp.int32)
        _lenS2 = 77 - jax.random.randint(jax.random.fold_in(_rk, 8), (4,), 0, max(1, 77 // 4) + 1, jnp.int32)
        _ctx_1024P = jax.random.normal(jax.random.fold_in(_rk, 11), (4, 16, 128), jnp.float32)
        _ctx_1024c = jax.random.dirichlet(jax.random.fold_in(_rk, 511), 0.3 * jnp.ones((16,), jnp.float32), (4, 77))
        _ctx_1024t = jnp.einsum('bsk,bkd->bsd', _ctx_1024c, _ctx_1024P)
        _ctx_1024t = _ctx_1024t * jax.lax.rsqrt(jnp.mean(jnp.square(_ctx_1024t)) + 1e-12) * 0.953939
        ctx_1024 = 4.13588e-05 + 0.999923 * (_ctx_1024t + 0.3 * jax.random.normal(jax.random.fold_in(_rk, 611), (4, 77, 128), jnp.float32))
        _validS = jnp.arange(512)[None, :] < _lenS[:, None]
        _validS2 = jnp.arange(77)[None, :] < _lenS2[:, None]
        _causal = jnp.tril(jnp.ones((512, 512), dtype=bool))
        mask_Bx1xSxS2_bk1 = jnp.broadcast_to(_validS2[:, None, None, :], (4, 1, 512, 77))
        mask_BxS2_ik0 = jnp.where(jnp.broadcast_to(_validS2[:, :], (4, 77)), 0, 1).astype(jnp.int32)
        mask_1x1xSxS2_bk0 = jnp.logical_not(jnp.broadcast_to(_validS2[0:1, None, None, :], (1, 1, 512, 77)))
        return (x, ctx_1024, mask_Bx1xSxS2_bk1, mask_BxS2_ik0, mask_1x1xSxS2_bk0)
    x, ctx_1024, mask_Bx1xSxS2_bk1, mask_BxS2_ik0, mask_1x1xSxS2_bk0 = _rec_inputs()

    def _L0_xattn_setup():
        import jax, jax.numpy as jnp
        import numpy as np
        B, S, D, H = (4, 256, 128, 16)
        HD = D // H
        key = jax.random.key(seed)
        ks = jax.random.split(key, 12)
        scale = 1.0 / np.sqrt(D)
        inp = {'queries': jax.random.normal(ks[0], (B, S, D), jnp.float32), 'keys': jax.random.normal(ks[1], (B, S, D), jnp.float32), 'values': jax.random.normal(ks[2], (B, S, D), jnp.float32), 'mask': jax.random.randint(ks[3], (B, 1, S, S), 0, 2).astype(bool), 'Wq': jax.random.normal(ks[4], (D, D), jnp.float32) * scale, 'bq': jnp.zeros((D,), jnp.float32), 'Wk': jax.random.normal(ks[5], (D, D), jnp.float32) * scale, 'bk': jnp.zeros((D,), jnp.float32), 'Wv': jax.random.normal(ks[6], (D, D), jnp.float32) * scale, 'bv': jnp.zeros((D,), jnp.float32), 'Wo': jax.random.normal(ks[7], (D, D), jnp.float32) * scale, 'bo': jnp.zeros((D,), jnp.float32)}
        return inp
    _L0_xattn_all = _L0_xattn_setup()
    _L0_xattn_in = {k: v for k, v in _L0_xattn_all.items() if k in ('Wq', 'bq', 'Wk', 'bk', 'Wv', 'bv', 'Wo', 'bo')}
    del _L0_xattn_all

    def _L0_ffn_setup():
        import jax, jax.numpy as jnp
        import numpy as np
        E = 8
        K = 2
        C = 128
        F = 256
        EPS = 1e-05
        key = jax.random.key(seed)
        ks = jax.random.split(key, 6)
        x = jax.random.normal(ks[0], (2, 128, C), dtype=jnp.float32)
        ln_gamma = 1.0 + 0.02 * jax.random.normal(ks[1], (C,), dtype=jnp.float32)
        ln_beta = 0.02 * jax.random.normal(ks[2], (C,), dtype=jnp.float32)
        gate_w = jax.random.normal(ks[3], (E, C), dtype=jnp.float32) / np.sqrt(C)
        w1 = jax.random.normal(ks[4], (E, F, C), dtype=jnp.float32) / np.sqrt(C)
        w2 = jax.random.normal(ks[5], (E, C, F), dtype=jnp.float32) / np.sqrt(F)
        return {'x': x, 'ln_gamma': ln_gamma, 'ln_beta': ln_beta, 'gate_w': gate_w, 'w1': w1, 'w2': w2}
    _L0_ffn_all = _L0_ffn_setup()
    _L0_ffn_in = {k: v for k, v in _L0_ffn_all.items() if k in ('ln_gamma', 'ln_beta', 'gate_w', 'w1', 'w2')}
    del _L0_ffn_all

    def _L1_xattn_setup():
        import jax, jax.numpy as jnp
        import numpy as np
        B, LQ, LK, D = (4, 256, 256, 128)
        H = 16
        HD = D // H

        def _split_heads(x):
            b, l, _ = x.shape
            return x.reshape(b, l, H, HD).transpose(0, 2, 1, 3)
        key = jax.random.key(seed)
        ks = jax.random.split(key, 10)
        s = 0.02
        return {'hidden_states': jax.random.normal(ks[0], (B, LQ, D), jnp.float32), 'context': jax.random.normal(ks[1], (B, LK, D), jnp.float32), 'attention_mask': jax.random.randint(ks[2], (B, LK), 0, 2, jnp.int32), 'q_w': jax.random.normal(ks[3], (D, D), jnp.float32) * s, 'q_b': jnp.zeros((D,), jnp.float32), 'k_w': jax.random.normal(ks[4], (D, D), jnp.float32) * s, 'k_b': jnp.zeros((D,), jnp.float32), 'v_w': jax.random.normal(ks[5], (D, D), jnp.float32) * s, 'v_b': jnp.zeros((D,), jnp.float32)}
    _L1_xattn_all = _L1_xattn_setup()
    _L1_xattn_in = {k: v for k, v in _L1_xattn_all.items() if k in ('q_w', 'q_b', 'k_w', 'k_b', 'v_w', 'v_b')}
    del _L1_xattn_all

    def _L1_ffn_setup():
        import jax, jax.numpy as jnp
        import numpy as np
        NUM_EXPERTS = 8
        HIDDEN = 128
        FFN = 512
        BATCH = 2
        SEQ = 256
        key = jax.random.key(seed)
        k_x, k_g, k_u, k_d = jax.random.split(key, 4)
        scale_in = 1.0 / np.sqrt(HIDDEN)
        scale_mid = 1.0 / np.sqrt(FFN)
        return {'hidden_states': jax.random.normal(k_x, (BATCH, SEQ, HIDDEN), dtype=jnp.float32), 'Wg': jax.random.normal(k_g, (NUM_EXPERTS, HIDDEN, FFN), dtype=jnp.float32) * scale_in, 'Wu': jax.random.normal(k_u, (NUM_EXPERTS, HIDDEN, FFN), dtype=jnp.float32) * scale_in, 'Wd': jax.random.normal(k_d, (NUM_EXPERTS, FFN, HIDDEN), dtype=jnp.float32) * scale_mid}
    _L1_ffn_all = _L1_ffn_setup()
    _L1_ffn_in = {k: v for k, v in _L1_ffn_all.items() if k in ('Wg', 'Wu', 'Wd')}
    del _L1_ffn_all

    def _L2_xattn_setup():
        import jax, jax.numpy as jnp
        import numpy as np
        EMBED_DIM = 128
        HEADS = 16
        D_HEAD = EMBED_DIM // HEADS
        B, S = (2, 256)
        key = jax.random.key(seed)
        ks = jax.random.split(key, 7)
        scale = 1.0 / np.sqrt(EMBED_DIM)
        inp = {'key': jax.random.normal(ks[0], (B, S, EMBED_DIM), dtype=jnp.float32), 'query': jax.random.normal(ks[1], (B, S, EMBED_DIM), dtype=jnp.float32), 'value': jax.random.normal(ks[2], (B, S, EMBED_DIM), dtype=jnp.float32), 'mask': jnp.tril(jnp.ones((S, S), dtype=bool))[None, None, :, :], 'Wq': jax.random.normal(ks[3], (EMBED_DIM, EMBED_DIM), dtype=jnp.float32) * scale, 'Wk': jax.random.normal(ks[4], (EMBED_DIM, EMBED_DIM), dtype=jnp.float32) * scale, 'Wv': jax.random.normal(ks[5], (EMBED_DIM, EMBED_DIM), dtype=jnp.float32) * scale, 'Wo': jax.random.normal(ks[6], (EMBED_DIM, EMBED_DIM), dtype=jnp.float32) * scale}
        return inp
    _L2_xattn_all = _L2_xattn_setup()
    _L2_xattn_in = {k: v for k, v in _L2_xattn_all.items() if k in ('Wq', 'Wk', 'Wv', 'Wo')}
    del _L2_xattn_all

    def _L2_ffn_setup():
        import jax, jax.numpy as jnp
        import numpy as np
        H = 128
        I = 4 * H
        E = 8
        TOP_K = 2
        key = jax.random.key(seed)
        ks = jax.random.split(key, 6)
        s = 0.02
        hidden_states = jax.random.normal(ks[0], (4, 512, H), dtype=jnp.float32)
        w1_shared = jax.random.normal(ks[1], (H, I), dtype=jnp.float32) * s
        w2_shared = jax.random.normal(ks[2], (I, H), dtype=jnp.float32) * s
        w1_routed = jax.random.normal(ks[3], (E, H, I), dtype=jnp.float32) * s
        w2_routed = jax.random.normal(ks[4], (E, I, H), dtype=jnp.float32) * s
        w_router = jax.random.normal(ks[5], (H, E), dtype=jnp.float32) * s
        return {'hidden_states': hidden_states, 'w1_shared': w1_shared, 'w2_shared': w2_shared, 'w1_routed': w1_routed, 'w2_routed': w2_routed, 'w_router': w_router}
    _L2_ffn_all = _L2_ffn_setup()
    _L2_ffn_in = {k: v for k, v in _L2_ffn_all.items() if k in ('w1_shared', 'w2_shared', 'w1_routed', 'w2_routed', 'w_router')}
    del _L2_ffn_all

    def _L3_xattn_setup():
        import jax, jax.numpy as jnp
        import numpy as np
        B, M, N, DIM, DH, H = (8, 512, 64, 128, 128, 8)
        INNER = DH * H
        EPS = 1e-05

        def _layernorm(x, g, b):
            mu = jnp.mean(x, axis=-1, keepdims=True)
            var = jnp.var(x, axis=-1, keepdims=True)
            return (x - mu) * jax.lax.rsqrt(var + EPS) * g + b
        key = jax.random.key(seed)
        ks = jax.random.split(key, 8)
        sd = 0.02
        return {'x': jax.random.normal(ks[0], (B, M, DIM), jnp.float32), 'latents': jax.random.normal(ks[1], (B, N, DIM), jnp.float32), 'gamma_media': jnp.ones((DIM,), jnp.float32), 'beta_media': jnp.zeros((DIM,), jnp.float32), 'gamma_lat': jnp.ones((DIM,), jnp.float32), 'beta_lat': jnp.zeros((DIM,), jnp.float32), 'Wq': jax.random.normal(ks[2], (DIM, INNER), jnp.float32) * sd, 'bq': jnp.zeros((INNER,), jnp.float32), 'Wkv': jax.random.normal(ks[3], (DIM, 2 * INNER), jnp.float32) * sd, 'bkv': jnp.zeros((2 * INNER,), jnp.float32), 'Wo': jax.random.normal(ks[4], (INNER, DIM), jnp.float32) * sd, 'bo': jnp.zeros((DIM,), jnp.float32)}
    _L3_xattn_all = _L3_xattn_setup()
    _L3_xattn_in = {k: v for k, v in _L3_xattn_all.items() if k in ('gamma_media', 'beta_media', 'gamma_lat', 'beta_lat', 'Wq', 'bq', 'Wkv', 'bkv', 'Wo', 'bo')}
    del _L3_xattn_all

    def _L3_ffn_setup():
        import jax, jax.numpy as jnp
        import numpy as np
        TOP_K = 2
        key = jax.random.key(seed)
        ks = jax.random.split(key, 5)
        B, T, D, F, E = (4, 256, 128, 512, 8)
        s = 0.02
        return {'x': jax.random.normal(ks[0], (B, T, D), jnp.float32), 'gate_w': jax.random.normal(ks[1], (D, E), jnp.float32) * s, 'w1': jax.random.normal(ks[2], (E, D, F), jnp.float32) * s, 'w3': jax.random.normal(ks[3], (E, D, F), jnp.float32) * s, 'w2': jax.random.normal(ks[4], (E, F, D), jnp.float32) * s}
    _L3_ffn_all = _L3_ffn_setup()
    _L3_ffn_in = {k: v for k, v in _L3_ffn_all.items() if k in ('gate_w', 'w1', 'w3', 'w2')}
    del _L3_ffn_all
    return {'x': x, 'ctx_1024': ctx_1024, 'mask_Bx1xSxS2_bk1': mask_Bx1xSxS2_bk1, 'mask_BxS2_ik0': mask_BxS2_ik0, 'mask_1x1xSxS2_bk0': mask_1x1xSxS2_bk0, 'L0_xattn_Wq': _L0_xattn_in['Wq'], 'L0_xattn_bq': _L0_xattn_in['bq'], 'L0_xattn_Wk': _L0_xattn_in['Wk'], 'L0_xattn_bk': _L0_xattn_in['bk'], 'L0_xattn_Wv': _L0_xattn_in['Wv'], 'L0_xattn_bv': _L0_xattn_in['bv'], 'L0_xattn_Wo': _L0_xattn_in['Wo'], 'L0_xattn_bo': _L0_xattn_in['bo'], 'L0_ffn_ln_gamma': _L0_ffn_in['ln_gamma'], 'L0_ffn_ln_beta': _L0_ffn_in['ln_beta'], 'L0_ffn_gate_w': _L0_ffn_in['gate_w'], 'L0_ffn_w1': _L0_ffn_in['w1'], 'L0_ffn_w2': _L0_ffn_in['w2'], 'L1_xattn_q_w': _L1_xattn_in['q_w'], 'L1_xattn_q_b': _L1_xattn_in['q_b'], 'L1_xattn_k_w': _L1_xattn_in['k_w'], 'L1_xattn_k_b': _L1_xattn_in['k_b'], 'L1_xattn_v_w': _L1_xattn_in['v_w'], 'L1_xattn_v_b': _L1_xattn_in['v_b'], 'L1_ffn_Wg': _L1_ffn_in['Wg'], 'L1_ffn_Wu': _L1_ffn_in['Wu'], 'L1_ffn_Wd': _L1_ffn_in['Wd'], 'L2_xattn_Wq': _L2_xattn_in['Wq'], 'L2_xattn_Wk': _L2_xattn_in['Wk'], 'L2_xattn_Wv': _L2_xattn_in['Wv'], 'L2_xattn_Wo': _L2_xattn_in['Wo'], 'L2_ffn_w1_shared': _L2_ffn_in['w1_shared'], 'L2_ffn_w2_shared': _L2_ffn_in['w2_shared'], 'L2_ffn_w1_routed': _L2_ffn_in['w1_routed'], 'L2_ffn_w2_routed': _L2_ffn_in['w2_routed'], 'L2_ffn_w_router': _L2_ffn_in['w_router'], 'L3_xattn_gamma_media': _L3_xattn_in['gamma_media'], 'L3_xattn_beta_media': _L3_xattn_in['beta_media'], 'L3_xattn_gamma_lat': _L3_xattn_in['gamma_lat'], 'L3_xattn_beta_lat': _L3_xattn_in['beta_lat'], 'L3_xattn_Wq': _L3_xattn_in['Wq'], 'L3_xattn_bq': _L3_xattn_in['bq'], 'L3_xattn_Wkv': _L3_xattn_in['Wkv'], 'L3_xattn_bkv': _L3_xattn_in['bkv'], 'L3_xattn_Wo': _L3_xattn_in['Wo'], 'L3_xattn_bo': _L3_xattn_in['bo'], 'L3_ffn_gate_w': _L3_ffn_in['gate_w'], 'L3_ffn_w1': _L3_ffn_in['w1'], 'L3_ffn_w3': _L3_ffn_in['w3'], 'L3_ffn_w2': _L3_ffn_in['w2']}

def reference(x, ctx_1024, mask_Bx1xSxS2_bk1, mask_BxS2_ik0, mask_1x1xSxS2_bk0, L0_xattn_Wq, L0_xattn_bq, L0_xattn_Wk, L0_xattn_bk, L0_xattn_Wv, L0_xattn_bv, L0_xattn_Wo, L0_xattn_bo, L0_ffn_ln_gamma, L0_ffn_ln_beta, L0_ffn_gate_w, L0_ffn_w1, L0_ffn_w2, L1_xattn_q_w, L1_xattn_q_b, L1_xattn_k_w, L1_xattn_k_b, L1_xattn_v_w, L1_xattn_v_b, L1_ffn_Wg, L1_ffn_Wu, L1_ffn_Wd, L2_xattn_Wq, L2_xattn_Wk, L2_xattn_Wv, L2_xattn_Wo, L2_ffn_w1_shared, L2_ffn_w2_shared, L2_ffn_w1_routed, L2_ffn_w2_routed, L2_ffn_w_router, L3_xattn_gamma_media, L3_xattn_beta_media, L3_xattn_gamma_lat, L3_xattn_beta_lat, L3_xattn_Wq, L3_xattn_bq, L3_xattn_Wkv, L3_xattn_bkv, L3_xattn_Wo, L3_xattn_bo, L3_ffn_gate_w, L3_ffn_w1, L3_ffn_w3, L3_ffn_w2):
    import jax
    import jax.numpy as jnp

    def _L0_xattn_ref(queries, keys, values, mask, Wq, bq, Wk, bk, Wv, bv, Wo, bo):
        import jax, jax.numpy as jnp
        import numpy as np
        B, S, D, H = (4, 256, 128, 16)
        HD = D // H
        b, sq, d = queries.shape

        def split_heads(x):
            return x.reshape(b, x.shape[1], H, HD).transpose(0, 2, 1, 3)
        q = split_heads(queries @ Wq + bq)
        k = split_heads(keys @ Wk + bk)
        v = split_heads(values @ Wv + bv)
        scores = jnp.einsum('bhqd,bhkd->bhqk', q, k) / jnp.sqrt(jnp.float32(HD))
        scores = jnp.where(mask, jnp.float32(-1000000000000000.0), scores)
        attn = jax.nn.softmax(scores, axis=-1)
        ctx = jnp.einsum('bhqk,bhkd->bhqd', attn, v)
        ctx = ctx.transpose(0, 2, 1, 3).reshape(b, sq, d)
        return ctx @ Wo + bo

    def _L0_ffn_ref(x, ln_gamma, ln_beta, gate_w, w1, w2):
        import jax, jax.numpy as jnp
        import numpy as np
        E = 8
        K = 2
        C = 128
        F = 256
        EPS = 1e-05
        B, T, Cc = x.shape
        xf = x.reshape(-1, Cc)
        mu = jnp.mean(xf, axis=-1, keepdims=True)
        var = jnp.var(xf, axis=-1, keepdims=True)
        rn = (xf - mu) * jax.lax.rsqrt(var + EPS) * ln_gamma + ln_beta
        logits = rn @ gate_w.T
        probs = jax.nn.softmax(logits, axis=-1)
        rw, sel = jax.lax.top_k(probs, K)
        comb = jnp.sum(jax.nn.one_hot(sel, E, dtype=xf.dtype) * rw[..., None], axis=1)
        h = jax.nn.gelu(jnp.einsum('nc,efc->enf', xf, w1), approximate=False)
        y = jnp.einsum('enf,ecf->enc', h, w2)
        out = jnp.einsum('enc,ne->nc', y, comb)
        return out.reshape(B, T, Cc)

    def _L1_xattn_ref(hidden_states, context, attention_mask, q_w, q_b, k_w, k_b, v_w, v_b):
        import jax, jax.numpy as jnp
        import numpy as np
        B, LQ, LK, D = (4, 256, 256, 128)
        H = 16
        HD = D // H

        def _split_heads(x):
            b, l, _ = x.shape
            return x.reshape(b, l, H, HD).transpose(0, 2, 1, 3)
        q = _split_heads(hidden_states @ q_w.T + q_b)
        k = _split_heads(context @ k_w.T + k_b)
        v = _split_heads(context @ v_w.T + v_b)
        scores = jnp.einsum('bhqd,bhkd->bhqk', q, k) / jnp.sqrt(jnp.float32(HD))
        mask = (attention_mask > 0)[:, None, None, :]
        scores = jnp.where(mask, -jnp.inf, scores)
        probs = jax.nn.softmax(scores, axis=-1)
        ctx = jnp.einsum('bhqk,bhkd->bhqd', probs, v)
        ctx = ctx.transpose(0, 2, 1, 3).reshape(ctx.shape[0], ctx.shape[2], H * HD)
        return ctx

    def _L1_ffn_ref(hidden_states, Wg, Wu, Wd):
        import jax, jax.numpy as jnp
        import numpy as np
        NUM_EXPERTS = 8
        HIDDEN = 128
        FFN = 512
        BATCH = 2
        SEQ = 256
        B, S, H = hidden_states.shape
        x = hidden_states.reshape(-1, H)

        def expert_step(acc, w):
            wg, wu, wd = w
            h = jax.nn.silu(x @ wg) * (x @ wu)
            return (acc + h @ wd, None)
        acc, _ = jax.lax.scan(expert_step, jnp.zeros_like(x), (Wg, Wu, Wd))
        return acc.reshape(B, S, H)

    def _L2_xattn_ref(key, query, value, mask, Wq, Wk, Wv, Wo):
        import jax, jax.numpy as jnp
        import numpy as np
        EMBED_DIM = 128
        HEADS = 16
        D_HEAD = EMBED_DIM // HEADS
        B, S = (2, 256)
        b, sq, _ = query.shape
        sk = key.shape[1]
        q = (query @ Wq.T).reshape(b, sq, HEADS, D_HEAD).transpose(0, 2, 1, 3)
        k = (key @ Wk.T).reshape(b, sk, HEADS, D_HEAD).transpose(0, 2, 1, 3)
        v = (value @ Wv.T).reshape(b, sk, HEADS, D_HEAD).transpose(0, 2, 1, 3)
        scores = jnp.einsum('bhqd,bhkd->bhqk', q, k) / jnp.sqrt(jnp.float32(D_HEAD))
        scores = jnp.where(mask, scores, jnp.float32(-1000000000.0))
        attn = jax.nn.softmax(scores, axis=-1)
        out = jnp.einsum('bhqk,bhkd->bhqd', attn, v)
        out = out.transpose(0, 2, 1, 3).reshape(b, sq, EMBED_DIM)
        return out @ Wo.T

    def _L2_ffn_ref(hidden_states, w1_shared, w2_shared, w1_routed, w2_routed, w_router):
        import jax, jax.numpy as jnp
        import numpy as np
        H = 128
        I = 4 * H
        E = 8
        TOP_K = 2
        bsz, seq_len, hidden_dim = hidden_states.shape
        flat = hidden_states.reshape(-1, hidden_dim)
        shared_out = jax.nn.silu(flat @ w1_shared) @ w2_shared
        router_logits = flat @ w_router
        routing_weights = jax.nn.softmax(router_logits, axis=-1)
        topk_w, topk_idx = jax.lax.top_k(routing_weights, TOP_K)
        topk_w = topk_w / jnp.sum(topk_w, axis=-1, keepdims=True)
        one_hot = jax.nn.one_hot(topk_idx, E, dtype=topk_w.dtype)
        cw = jnp.einsum('tk,tke->te', topk_w, one_hot)
        routed_out = jnp.zeros_like(flat)
        for e in range(E):
            expert_out = jax.nn.silu(flat @ w1_routed[e]) @ w2_routed[e]
            routed_out = routed_out + cw[:, e:e + 1] * expert_out
        total = shared_out + routed_out
        return total.reshape(bsz, seq_len, hidden_dim)

    def _L3_xattn_ref(x, latents, gamma_media, beta_media, gamma_lat, beta_lat, Wq, bq, Wkv, bkv, Wo, bo):
        import jax, jax.numpy as jnp
        import numpy as np
        B, M, N, DIM, DH, H = (8, 512, 64, 128, 128, 8)
        INNER = DH * H
        EPS = 1e-05

        def _layernorm(x, g, b):
            mu = jnp.mean(x, axis=-1, keepdims=True)
            var = jnp.var(x, axis=-1, keepdims=True)
            return (x - mu) * jax.lax.rsqrt(var + EPS) * g + b
        b = x.shape[0]
        xn = _layernorm(x, gamma_media, beta_media)
        ln = _layernorm(latents, gamma_lat, beta_lat)
        q = ln @ Wq + bq
        kv_input = jnp.concatenate([xn, ln], axis=1)
        kv = kv_input @ Wkv + bkv
        k, v = jnp.split(kv, 2, axis=-1)

        def to_heads(t):
            return t.reshape(b, t.shape[1], H, DH).transpose(0, 2, 1, 3)
        q, k, v = (to_heads(q), to_heads(k), to_heads(v))
        q = q * DH ** (-0.5)
        sim = jnp.einsum('bhid,bhjd->bhij', q, k)
        attn = jax.nn.softmax(sim, axis=-1)
        out = jnp.einsum('bhij,bhjd->bhid', attn, v)
        out = out.transpose(0, 2, 1, 3).reshape(b, -1, INNER)
        return out @ Wo + bo

    def _L3_ffn_ref(x, gate_w, w1, w3, w2):
        import jax, jax.numpy as jnp
        import numpy as np
        TOP_K = 2
        logits = jnp.einsum('btd,de->bte', x, gate_w)
        probs = jax.nn.softmax(logits, axis=-1)
        expert_weights, expert_indices = jax.lax.top_k(probs, TOP_K)
        expert_weights = expert_weights / expert_weights.sum(-1, keepdims=True)
        E = w1.shape[0]
        out = jnp.zeros_like(x)
        for i in range(E):
            wi = jnp.where(expert_indices == i, expert_weights, 0.0).sum(-1)
            h = jax.nn.silu(jnp.einsum('btd,df->btf', x, w1[i])) * jnp.einsum('btd,df->btf', x, w3[i])
            out = out + jnp.einsum('btf,fd->btd', h, w2[i]) * wi[..., None]
        return out
    x = x + _L0_xattn_ref(_layernorm(x, axis=-1), ctx_1024, ctx_1024, mask_Bx1xSxS2_bk1, L0_xattn_Wq, L0_xattn_bq, L0_xattn_Wk, L0_xattn_bk, L0_xattn_Wv, L0_xattn_bv, L0_xattn_Wo, L0_xattn_bo)
    x = x + _L0_ffn_ref(_layernorm(x, axis=-1), L0_ffn_ln_gamma, L0_ffn_ln_beta, L0_ffn_gate_w, L0_ffn_w1, L0_ffn_w2)
    x = x + _L1_xattn_ref(_layernorm(x, axis=-1), ctx_1024, mask_BxS2_ik0, L1_xattn_q_w, L1_xattn_q_b, L1_xattn_k_w, L1_xattn_k_b, L1_xattn_v_w, L1_xattn_v_b)
    x = x + _L1_ffn_ref(_layernorm(x, axis=-1), L1_ffn_Wg, L1_ffn_Wu, L1_ffn_Wd)
    x = x + _L2_xattn_ref(ctx_1024, _layernorm(x, axis=-1), ctx_1024, mask_1x1xSxS2_bk0, L2_xattn_Wq, L2_xattn_Wk, L2_xattn_Wv, L2_xattn_Wo)
    x = x + _L2_ffn_ref(_layernorm(x, axis=-1), L2_ffn_w1_shared, L2_ffn_w2_shared, L2_ffn_w1_routed, L2_ffn_w2_routed, L2_ffn_w_router)
    x = x + _L3_xattn_ref(ctx_1024, _layernorm(x, axis=-1), L3_xattn_gamma_media, L3_xattn_beta_media, L3_xattn_gamma_lat, L3_xattn_beta_lat, L3_xattn_Wq, L3_xattn_bq, L3_xattn_Wkv, L3_xattn_bkv, L3_xattn_Wo, L3_xattn_bo)
    x = x + _L3_ffn_ref(_layernorm(x, axis=-1), L3_ffn_gate_w, L3_ffn_w1, L3_ffn_w3, L3_ffn_w2)
    return x

_drawn_inputs = setup_inputs


def setup_inputs(seed=0):
    import zlib

    import numpy as np

    out = dict(_drawn_inputs(seed))
    spreads = {'L0_xattn_bq': (0.0, 0.1),
     'L0_xattn_bk': (0.0, 0.8),
     'L0_xattn_bv': (0.0, 0.1),
     'L0_xattn_bo': (0.0, 0.1),
     'L1_xattn_q_b': (0.0, 0.8),
     'L1_xattn_k_b': (0.0, 0.8),
     'L1_xattn_v_b': (0.0, 0.1),
     'L3_xattn_gamma_media': (1.0, 0.6),
     'L3_xattn_beta_media': (0.0, 0.8),
     'L3_xattn_gamma_lat': (1.0, 0.6),
     'L3_xattn_beta_lat': (0.0, 0.8),
     'L3_xattn_bq': (0.0, 0.8),
     'L3_xattn_bkv': (0.0, 0.278),
     'L3_xattn_bo': (0.0, 0.1)}
    factors = {'L0_ffn_ln_gamma': 3.027,
     'L1_xattn_q_w': 8.0,
     'L1_xattn_k_w': 8.0,
     'L2_ffn_w1_routed': 3.484,
     'L2_ffn_w2_routed': 3.474,
     'L2_ffn_w_router': 4.038,
     'L3_xattn_Wq': 8.0,
     'L3_ffn_gate_w': 8.0,
     'L3_ffn_w1': 8.0,
     'L3_ffn_w3': 8.0,
     'L3_ffn_w2': 8.0}
    for name, (base, spread) in spreads.items():
        noise = np.random.default_rng([zlib.crc32(name.encode()), seed]).standard_normal(out[name].shape)
        drawn = base * np.exp(spread * noise) if base else spread * noise
        out[name] = jnp.asarray(drawn.astype(out[name].dtype))
    for name, factor in factors.items():
        out[name] = (out[name] * factor).astype(out[name].dtype)
    return out
```

```python
import concourse.bass as bass
from concourse import mybir
from contextlib import ExitStack

PHASES = 8

B, S, D = 4, 512, 128
KC = 77
P = 128
NT = B * S // P
TB = 4
NB = NT // TB
EPS = 1e-5
NE = 8
H, HD = 16, 8
HG = 4
NG = H // HG
GW = HG * KC
NCH = 3
CH = -(-GW // NCH)
GWP = NCH * CH
VC = HD + 1
NEG = -1e30
LH, LD = 8, 128
KEYS = S + KC
KP = KC + 1
XS = 4
CREDIT = 4096


class Experts:
    pass


def build(nc, x_in, ctx_t, ctx_rows, mask0, mask1, mask2, attn_w, cols, rows, gates,
          f0, f1, f2, f3, xw, xcols, out):
    f32, f32r, bf16 = mybir.dt.float32, mybir.dt.float32r, mybir.dt.bfloat16
    i32, u8 = mybir.dt.int32, mybir.dt.uint8
    ALU = mybir.AluOpType
    ACT = mybir.ActivationFunctionType
    AX = mybir.AxisListType
    ds = bass.ds

    stack = ExitStack()
    with stack:
        def sb(name, shape, dt=f32):
            return stack.enter_context(nc.sbuf_tensor(name, shape, dt))

        def sem(name):
            return stack.enter_context(nc.semaphore(name))

        psum = stack.enter_context(nc.psum_tensor("psum", [P, 8 * 512], f32))

        def bank(n, width=512):
            return psum[:, n * 512:n * 512 + width]

        x = sb("x", [P, NT, D])
        xh = sb("xh", [P, NT * P], f32r)
        xl = sb("xl", [P, NT * P], f32r)
        xn = sb("xn", [P, NT, D])
        ident = sb("ident", [P, P])
        identb = sb("identb", [P, P], bf16)
        ones_row = sb("ones_row", [1, P])
        stats = sb("stats", [P, NT, 6])
        mv = sb("mv", [P, NT, 2])
        vpe = sb("vpe", [P, NT])
        nhv = sb("nhv", [P, NT])
        seed = sb("seed", [P, NT], i32)
        rstd = sb("rstd", [P, NT])
        rtmp = sb("rtmp", [P, NT])
        rstd2 = sb("rstd2", [P, NT])
        ctxT = sb("ctxT", [P, B * KC])
        aw = sb("aw", [P, 11 * P])
        wqh = sb("wqh", [P, 3 * P], f32r)
        wql = sb("wql", [P, 3 * P], f32r)
        pcols = sb("pcols", [P, 8])
        prows = sb("prows", [P, 3, D])
        worow = sb("worow", [1, D])
        kh = sb("kh", [P, 3, B * KC], f32r)
        kl = sb("kl", [P, 3, B * KC], f32r)
        vall = sb("vall", [KC, 3, B * D])
        hmask = sb("hmask", [P, H])
        cmask = sb("cmask", [CH, NCH, NG, HG])
        spreadp = sb("spreadp", [KC, GWP])
        spread = spreadp[:, 0:GW].rearrange("k (h c) -> k h c", h=HG)
        kb = sb("kb", [P, 4 * H * KC], f32r)
        kbh = [kb[:, s * H * KC:(s + 1) * H * KC] for s in range(2)]
        kbl = [kb[:, (2 + s) * H * KC:(3 + s) * H * KC] for s in range(2)]
        vx = [sb(f"vx{s}", [CH, NCH, H, VC]) for s in range(2)]
        qh = [sb(f"qh{s}", [P, S], f32r) for s in range(2)]
        ql = [sb(f"ql{s}", [P, S], f32r) for s in range(2)]
        maskneg = sb("maskneg", [P, 3, NT, KC], bf16)
        seen = sb("seen", [P, B])
        smax = sb("smax", [P, 2, HG])
        shared = sb("shared", [P, 3 * NT * P])
        m0u = shared[:, 0:NT * KC // 4].bitcast(u8).rearrange("p (t k) -> p t k", k=KC)
        m1i = shared[:, 512:512 + B * KC].bitcast(i32).rearrange("p (b k) -> p b k", k=KC)
        m1f = shared[:, 1024:1024 + B * KC].rearrange("p (b k) -> p b k", k=KC)
        m2u = shared[:, 1536:1536 + TB * KC // 4].bitcast(u8).rearrange("p (t k) -> p t k", k=KC)
        shifted = [shared[:, s * NG * GW:(s + 1) * NG * GW].rearrange("p (g k) -> p g k", g=NG)
                   for s in range(2)]
        probs = [shared[:, 2 * NG * GW + s * NG * GWP:2 * NG * GW + (s + 1) * NG * GWP]
                 .rearrange("p (g k) -> p g k", g=NG) for s in range(2)]
        pT = [sb(f"pT{s}", [CH, NCH * P]) for s in range(2)]
        rden = sb("rden", [P, H])
        onorm = [sb(f"onorm{s}", [P, H, HD]) for s in range(2)]
        wraw = sb("wraw", [P, 3072])
        kf = wraw[:, 2560:2560 + B * KC]
        wh = sb("wh", [P, 3072], f32r)
        wl = sb("wl", [P, 3072], f32r)
        act_out = [sb(f"act_out{s}", [P, 512]) for s in range(2)]
        qf = act_out[0][:, :]
        oT = sb("oT", [P, P])[:, :]
        hhl = sb("hhl", [P, 8 * 512], f32r)
        hh = [hhl[:, s * 512:(s + 1) * 512] for s in range(4)]
        hl = [hhl[:, (4 + s) * 512:(5 + s) * 512] for s in range(4)]
        yacc = xn[:, :, :].rearrange("p t d -> p (t d)")
        combs = [shared[:, s * NT * P:(s + 1) * NT * P] for s in range(3)]
        gw = sb("gw", [P, 3, NE])
        gwg = sb("gwg", [P, NE])
        gh = sb("gh", [P, 3, NE], f32r)
        gl = sb("gl", [P, 3, NE], f32r)
        betaB = sb("betaB", [P, P])
        gbias = sb("gbias", [P, NE])
        logits = sb("logits", [P, NT, NE])
        lmax = sb("lmax", [P, NT])
        lsub = sb("lsub", [P, NT, NE])
        lexp = sb("lexp", [P, NT, NE])
        tri = sb("tri", [P, NE, NE])
        above = xn[:, 0:TB * 2, :].rearrange("p t d -> p (t d)").rearrange("p (t a b) -> p t a b", a=NE, b=NE)
        tied = xn[:, TB * 2:, :].rearrange("p t d -> p (t d)").rearrange("p (t a b) -> p t a b", a=NE, b=NE)
        rank = sb("rank", [P, NT, NE])
        xc = sb("xc", [P, 3 * LH + 5])
        xcur = sb("xcur", [P, 3, 2])
        crow = wraw[0:KC, 2048:2048 + B * D].rearrange("k (b d) -> k b d", b=B)
        media = sb("media", [P, 2, B * KP], f32r)
        mh, ml = media[:, 0, :], media[:, 1, :]
        tails = [wl[:, 1024 + n * 512:1024 + (n + 1) * 512] for n in range(4)]
        xp4 = [[kb[:, 0:2048], kb[:, 2048:4096]], [hhl[:, 0:2048], hhl[:, 2048:4096]]]
        xp5 = [[kb[:, 4096:4608], tails[0]], [tails[1], tails[2]]]
        kxh = [wh[:, 1024 + s * 640:1024 + s * 640 + S + KP] for s in range(2)]
        kxl = [wh[:, 1024 + 2 * 640:1024 + 2 * 640 + S + KP], sb("kxl1", [P, S + KP], f32r)[:]]
        vxa = sb("vxa", [P, 2, 2, 5 * P], f32r)
        xsum = sb("xsum", [P, XS])
        xnm = sb("xnm", [P, XS])
        xrd = sb("xrd", [P, XS])
        xprob = [shared[:, s * 640:s * 640 + KEYS] for s in range(XS)]
        xdiag = [shared[:, XS * 640 + s * P:XS * 640 + (s + 1) * P] for s in range(XS)]
        xg = [shared[:, XS * 768 + s * 512:XS * 768 + (s + 1) * 512] for s in range(2)]
        oxh, oxl = [k[:, :, :].rearrange("p l k -> p (l k)")[:, 0:S] for k in (kh, kl)]
        wsum = sb("wsum", [P, NT])
        comb = sb("comb", [P, NT, NE])
        combT = xn[0:NE, :, :].rearrange("e t d -> e (t d)")
        one_rows = sb("one_rows", [NT, P])
        comb_dram = [nc.dram_tensor(f"comb_dram{n}", [NE + 1, NT * P], f32, kind="Internal").ap() for n in range(3)]

        x_loaded, ctx_loaded, small_loaded = sem("x_loaded"), sem("ctx_loaded"), sem("small_loaded")
        out_stored = sem("out_stored")
        consts = sem("consts")
        dve_step, act_step, pool_step = sem("dve_step"), sem("act_step"), sem("pool_step")
        xn_ready, xT_ps, xh_done, xl_done = sem("xn_ready"), sem("xT_ps"), sem("xh_done"), sem("xl_done")
        x_done = sem("x_done")
        k_ps, k_free, kh_done, kl_done = sem("k_ps"), sem("k_free"), sem("kh_done"), sem("kl_done")
        v_ps, v_done = sem("v_ps"), sem("v_done")
        wq_hi, wq_lo = sem("wq_hi"), sem("wq_lo")
        mask_done = sem("mask_done")
        q_ps, q_evac, qh_done, q_ready = sem("q_ps"), sem("q_evac"), sem("qh_done"), sem("q_ready")
        vx_ps, vx_ready, kb_ready = sem("vx_ps"), sem("vx_ready"), sem("kb_ready")
        s_ready, s_used, p_ready = sem("s_ready"), sem("s_used"), sem("p_ready")
        pt_ready, pt_done, pv_done = sem("pt_ready"), sem("pt_done"), sem("pv_done")
        o_used, ont_ready, ot_done, out_ready, x_upd = (
            sem("o_used"), sem("ont_ready"), sem("ot_done"), sem("out_ready"), sem("x_upd"))
        lg_ps, lsub_ready, lexp_ready, comb_ready, combT_ps, combT_done, comb_stored, gate_ps = (
            sem("lg_ps"), sem("lsub_ready"), sem("lexp_ready"), sem("comb_ready"), sem("combT_ps"),
            sem("combT_done"), sem("comb_stored"), sem("gate_ps"))
        xg_ready, med_ready, med_ps, med_hi, med_lo, med_f = (
            sem("xg_ready"), sem("med_ready"), sem("med_ps"), sem("med_hi"), sem("med_lo"), sem("med_f"))
        x_split, x_split_hi, x_scaled = sem("x_split"), sem("x_split_hi"), sem("x_scaled")
        xw_in = [sem(f"xw_in{s}") for s in range(2)]
        pj_ps, pj_hi, pj_lo = sem("pj_ps"), sem("pj_hi"), sem("pj_lo")
        xs_ready, xs_max, x_exp, x_rec, x_norm = (
            sem("xs_ready"), sem("xs_max"), sem("x_exp"), sem("x_rec"), sem("x_norm"))
        xt_ready, xt_hi, xt_lo = sem("xt_ready"), sem("xt_hi"), sem("xt_lo")
        xo_ready, xo_hi, xo_lo, xy_ready, xy_used = (
            sem("xo_ready"), sem("xo_hi"), sem("xo_lo"), sem("xy_ready"), sem("xy_used"))
        yT_ps, x_added, pool_turn, act_turn, xcur_ready = (
            sem("yT_ps"), sem("x_added"), sem("pool_turn"), sem("act_turn"), sem("xcur_ready"))

        class Steps:
            def __init__(self, eng, s):
                self.eng, self.sem, self.base, self.n = eng, s, 0, 0

            def link(self, ins):
                self.n += 1
                ins.then_inc(self.sem, 1)
                self.eng.wait_ge(self.sem, self.base + self.n)

            def enter(self, i, each):
                self.outer, self.each = self.base + self.n, each
                self.base, self.n = i * each + self.outer, 0

            def leave(self, times):
                assert self.n == self.each, (self.n, self.each)
                self.base, self.n = self.outer + times * self.each, 0

        def experts(name, index, route, w_dram, count, unroll, chunks, gated, func):
            f = Experts()
            f.name, f.index, f.route, f.w, f.E, f.U, f.nf, f.gated, f.func = (
                name, index, route, w_dram, count, unroll, chunks, gated, func)
            f.wc = chunks * P * (3 if gated else 2)
            f.iters = count // unroll
            f.NS = unroll * NB
            f.NK = f.NS * chunks
            f.w_in = [sem(f"{name}_w_in{s}") for s in range(unroll)]
            f.cb_in = [sem(f"{name}_cb_in{s}") for s in range(unroll)] if route is not None else None
            f.split = sem(f"{name}_split")
            f.wsplit_hi = sem(f"{name}_wsplit_hi")
            f.g_ready = sem(f"{name}_g_ready")
            f.g_used = sem(f"{name}_g_used")
            f.u_ready = sem(f"{name}_u_ready")
            f.hh_done = sem(f"{name}_hh_done")
            f.hf_done = sem(f"{name}_hf_done")
            f.h_ready = sem(f"{name}_h_ready")
            f.h_used = sem(f"{name}_h_used")
            f.y_used = sem(f"{name}_y_used")
            return f

        LAG = 3
        H_BANKS = (2, 3, 6, 7)

        def h_bank(f, k):
            return bank(H_BANKS[k % 4] if f.gated else k % 4)

        phases = []
        phases.append(("attn", 0))
        phases.append(("ffn", experts("f0", 1, 0, f0, NE, 2, 2, False, ACT.Gelu)))
        phases.append(("attn", 1))
        phases.append(("ffn", experts("f1", 3, None, f1, NE, 2, 4, True, ACT.Silu)))
        phases.append(("attn", 2))
        phases.append(("ffn", experts("f2", 5, 1, f2, NE + 1, 3, 4, False, ACT.Silu)))
        phases.append(("wide", None))
        phases.append(("ffn", experts("f3", 7, 2, f3, NE, 2, 4, True, ACT.Silu)))
        phases = phases[:PHASES]
        FF = {1: 0, 3: 1, 5: 2, 6: 3, 7: 4}

        block = stack.enter_context(nc.Block())

        def bcast(ap, n, at):
            ap = ap.unsqueeze(at)
            return ap.broadcast_to([n if d == at else size for d, size in enumerate(ap.shape)])

        @block.sync
        def _(sp):
            sp.dma_start(x[:], x_in.rearrange("b (t p) d -> p (b t) d", p=P)).then_inc(x_loaded, 16)
            sp.dma_start(ctxT[:], ctx_t).then_inc(ctx_loaded, 16)
            sp.dma_start(aw[:], attn_w).then_inc(ctx_loaded, 16)
            sp.dma_start(pcols[:], cols).then_inc(small_loaded, 16)
            sp.dma_start(prows[:, 0:2, :], bcast(rows[0:2, :], P, 0)).then_inc(small_loaded, 16)
            sp.dma_start(worow[:], rows[2:3, :]).then_inc(small_loaded, 16)
            sp.dma_start(xc[:], xcols).then_inc(small_loaded, 16)
            sp.dma_start(crow, ctx_rows.rearrange("b k d -> k b d")).then_inc(small_loaded, 16)
            sp.dma_start(gw[:], gates.rearrange("p (n e) -> p n e", n=3)).then_inc(small_loaded, 16)
            sp.dma_start(m0u, mask0.rearrange("b o (t p) k -> p (b o t) k", p=P)).then_inc(small_loaded, 16)
            sp.dma_start(m1i, bcast(mask1, P, 0)).then_inc(small_loaded, 16)
            sp.dma_start(m2u, mask2.rearrange("b o (t p) k -> p (b o t) k", p=P)).then_inc(small_loaded, 16)

            for kind, f in phases:
                if kind == "wide":
                    sp.wait_ge(x_done, 6)
                    with sp.Fori(0, LH // 2) as i:
                        for s in range(2):
                            sp.wait_ge(x_split, i * 2 + (s + 1))
                            sp.dma_start(wraw[:, s * 512:(s + 1) * 512],
                                         xw[ds(i * 2 + s, 1), :, :].rearrange("e p n -> p (e n)")
                                         ).then_inc(xw_in[s], 16)
                if kind != "ffn":
                    continue
                routed = f.route is not None
                if routed:
                    sp.wait_ge(combT_done, NB * (f.route + 1))
                    sp.dma_start(comb_dram[f.route][0:NE, :], combT[:]).then_inc(comb_stored, 16)
                    sp.dma_start(comb_dram[f.route][NE, :].rearrange("(a n) -> a n", n=P), one_rows[:]).then_inc(comb_stored, 16)
                    sp.wait_ge(comb_stored, 32 * (f.route + 1))
                if f.index > 1:
                    sp.wait_ge(x_done, 7 if f.index == 7 else f.index - 1)
                with sp.Fori(0, f.iters) as i:
                    for s in range(f.U):
                        sp.wait_ge(f.split, i * f.U + (s + 1))
                        sp.dma_start(wraw[:, s * f.wc:(s + 1) * f.wc],
                                     f.w[ds(i * f.U + s, 1), :, :].rearrange("e p n -> p (e n)")
                                     ).then_inc(f.w_in[s], 16)
                    for s in range(f.U if routed else 0):
                        sp.wait_ge(f.y_used, i * f.NS + (s + 1) * NB)
                        sp.dma_start(combs[s],
                                     comb_dram[f.route][ds(i * f.U + s, 1), :].broadcast_to([P, NT * P])).then_inc(f.cb_in[s], 16)
            sp.wait_ge(x_done, len(phases))
            sp.dma_start(out.rearrange("b (t p) d -> p (b t) d", p=P), x[:]).then_inc(out_stored, 16)
            sp.wait_ge(out_stored, 16)

        @block.gpsimd
        def _(pool):
            st = Steps(pool, pool_step)
            g = nc.gpsimd
            g.memset(ident[:], 0.0)
            g.memset(identb[:], 0.0)
            g.memset(ones_row[:], 1.0)
            g.memset(one_rows[:], 1.0)
            g.memset(hmask[:], 1.0)
            g.memset(cmask[:], 1.0)
            g.memset(spreadp[:], 0.0)
            g.memset(prows[:, 2, :], 0.0)
            st.link(g.memset(tri[:], 1.0))
            for m in (ident, identb):
                g.affine_select(out=m[:], in_=m[:], compare_op=ALU.not_equal, fill=1.0, base=0,
                                pattern=[[-1, P]], channel_multiplier=1)
            st.link(g.affine_select(out=hmask[:], in_=hmask[:], compare_op=ALU.is_ge, fill=0.0, base=0,
                                    pattern=[[-HD, H]], channel_multiplier=1))
            g.affine_select(out=hmask[:], in_=hmask[:], compare_op=ALU.is_ge, fill=0.0, base=HD - 1,
                            pattern=[[HD, H]], channel_multiplier=-1)
            for j in range(NCH):
                g.affine_select(out=cmask[:, j], in_=cmask[:, j], compare_op=ALU.is_ge, fill=0.0,
                                base=CH * j, pattern=[[0, NG], [-KC, HG]], channel_multiplier=1)
            st.link(g.affine_select(out=spread, in_=spread, compare_op=ALU.not_equal, fill=1.0, base=0,
                                    pattern=[[0, HG], [-1, KC]], channel_multiplier=1))
            for j in range(NCH):
                g.affine_select(out=cmask[:, j], in_=cmask[:, j], compare_op=ALU.is_ge, fill=0.0,
                                base=KC - 1 - CH * j, pattern=[[0, NG], [KC, HG]], channel_multiplier=-1)
            st.link(g.affine_select(out=tri[:], in_=tri[:], compare_op=ALU.is_ge, fill=0.0, base=-1,
                                    pattern=[[1, NE], [-1, NE]], channel_multiplier=0))
            for s in range(2):
                last = g.tensor_copy(vx[s][:, :, :, HD:VC],
                                     cmask[:].rearrange("r j g h -> r j (g h)").unsqueeze(3))
            last.then_inc(consts, 1)

            for kind, f in phases:
                if kind == "attn":
                    l = f
                    pool.wait_ge(kl_done, l + 1)
                    with pool.Fori(0, 2) as i:
                        for s in range(2):
                            it = i + 2 * l
                            pool.wait_ge(s_ready, it * 32 + (CREDIT + 16 * (s + 1) - 32))
                            for src, dst in ((kh, kbh), (kl, kbl)):
                                ins = g.tensor_tensor(
                                    out=dst[s].rearrange("p (h k) -> p h k", h=H),
                                    in0=bcast(src[:, l, ds(i * 2 * KC + s * KC, KC)].bitcast(f32), H, 1),
                                    in1=bcast(hmask[:], KC, 2), op=ALU.mult)
                            ins.then_inc(kb_ready, 1)
                elif kind == "wide":
                    pool.sem_inc(x_split, 2)
                    pool.wait_ge(x_done, 6)
                    with pool.Fori(0, LH // 2) as i:
                        def split(s):
                            raw, w = wraw[:, s * 512:(s + 1) * 512], slice(s * 512, (s + 1) * 512)
                            pool.wait_ge(xw_in[s], i * 16 + 16)
                            pool.wait_ge(xy_ready, i * 8 + 4 * (s + 1))
                            pool.sem_inc(pool_turn, 1)
                            g.tensor_scalar(raw[:, 0:P], raw[:, 0:P], LD ** -0.5, 1.0, ALU.mult, ALU.mult
                                            ).then_inc(x_scaled, 1)
                            pool.wait_ge(x_scaled, i * 2 + (s + 1))
                            pool.sem_inc(pool_turn, 1)
                            g.tensor_copy(wh[:, w], raw).then_inc(x_split_hi, 1)
                            pool.wait_ge(x_split_hi, i * 2 + (s + 1))
                            g.tensor_tensor(out=wl[:, w], in0=raw, in1=wh[:, w].bitcast(f32),
                                            op=ALU.subtract).then_inc(x_split, 1)

                        split(0)
                        split(1)
                else:
                    for s in range(f.U):
                        pool.sem_inc(f.split, 1)
                    if f.index > 1:
                        pool.wait_ge(x_done, 7 if f.index == 7 else f.index - 1)
                    with pool.Fori(0, f.iters) as i:
                        for s in range(f.U):
                            sl = slice(s * f.wc, (s + 1) * f.wc)
                            pool.wait_ge(f.w_in[s], i * 16 + 16)
                            pool.wait_ge(f.h_used, i * f.NK + (s + 1) * NB * f.nf)
                            pool.sem_inc(pool_turn, 1)
                            g.tensor_copy(wh[:, sl], wraw[:, sl]).then_inc(f.wsplit_hi, 1)
                            pool.wait_ge(f.wsplit_hi, i * f.U + (s + 1))
                            g.tensor_tensor(out=wl[:, sl], in0=wraw[:, sl], in1=wh[:, sl].bitcast(f32),
                                            op=ALU.subtract).then_inc(f.split, 1)

        @block.scalar
        def _(act):
            a = nc.scalar
            for l in range(3):
                act.wait_ge(k_free, l + 1)
                a.activation(kh[:, l, :], kf, ACT.Copy).then_inc(kh_done, 1)
            act.wait_ge(ctx_loaded, 32)
            for l, c in enumerate((0, 4, 7)):
                ins = a.activation(wqh[:, l * P:(l + 1) * P], aw[:, c * P:(c + 1) * P], ACT.Copy)
            ins.then_inc(wq_hi, 1)
            act.wait_ge(med_f, 1)
            a.activation(mh.rearrange("p (b k) -> p b k", b=B)[:, :, 0:KC],
                         xg[0][:, 0:B * KC].rearrange("p (b k) -> p b k", b=B), ACT.Copy).then_inc(med_hi, 1)

            for n, (kind, f) in enumerate(phases):
                for b in range(NB):
                    if kind == "wide":
                        act.wait_ge(xg_ready, b + 1)
                    else:
                        act.wait_ge(xT_ps, NB * n + b + 1)
                    a.activation(xh[:, b * 512:(b + 1) * 512], xg[b % 2] if kind == "wide" else bank(b), ACT.Copy
                                 ).then_inc(xh_done, 1)
                if kind == "wide":
                    with act.Fori(0, LH // 2) as i:
                        def high(u, part):
                            s, w = u % 2, i * 8 + u
                            e = u // NB
                            act.wait_ge(pj_ps, w * 4 + (part + 1))
                            if part == 0:
                                ins = a.activation(qh[s][:], bank(0), ACT.Identity, bias=xcur[:, 0, e:e + 1])
                            elif part == 1:
                                ins = a.activation(kxh[s][:, 0:S], bank(0), ACT.Identity,
                                                   bias=xcur[:, 1, e:e + 1])
                            elif part == 2:
                                a.activation(kxh[s][:, S:S + KP], bank(0, KP), ACT.Identity,
                                             bias=xcur[:, 1, e:e + 1])
                                ins = a.activation(vxa[0:KC, s, 0, 512:640], bank(0)[0:KC, 128:256], ACT.Copy)
                            else:
                                ins = a.activation(vxa[:, s, 0, 0:512], bank(0), ACT.Copy)
                            ins.then_inc(pj_hi, 1)

                        def softmax(m):
                            act.wait_ge(xs_max, i * 32 + (m + 1))
                            if m >= XS:
                                act.wait_ge(xt_ready, i * 32 + (m - XS + 1))
                            z = slice(m % XS, m % XS + 1)
                            a.activation(xprob[m % XS], bank(2 + 2 * (m % 2), KEYS), ACT.Exp,
                                         bias=xnm[:, z], accum_out=xsum[:, z]).then_inc(x_exp, 1)

                        def turned(m):
                            u, qt = m // 4, m % 4
                            act.wait_ge(xt_ready, i * 32 + (m + 1))
                            if u >= 2:
                                act.wait_ge(xo_ready, i * 8 + (u - 1))
                            a.activation(xp4[u % 2][0].rearrange("p (j q) -> p j q", j=4)[:, :, qt * P:(qt + 1) * P],
                                         bank(6).rearrange("p (j q) -> p j q", j=4), ACT.Copy)
                            a.activation(xp5[u % 2][0][0:KC, qt * P:(qt + 1) * P], bank(7)[0:KC, 0:P], ACT.Copy
                                         ).then_inc(xt_hi, 1)

                        def attended(u):
                            act.wait_ge(xo_ready, i * 8 + (u + 1))
                            a.activation(oxh, bank(1), ACT.Identity,
                                         bias=xcur[:, 2, u // NB:u // NB + 1]).then_inc(xo_hi, 1)

                        act.sem_inc(act_turn, 1)
                        a.activation(xcur[:], xc[:, 0:3 * LH].rearrange("p (c h) -> p c h", h=LH)[:, :, ds(i * 2, 2)],
                                     ACT.Copy).then_inc(xcur_ready, 1)
                        act.wait_ge(xcur_ready, i + 1)
                        for part in range(4):
                            high(0, part)
                        for u in range(8 + 1):
                            for qt in range(4):
                                m = 4 * u + qt
                                if 2 <= m < 34:
                                    turned(m - 2)
                                if m < 32:
                                    softmax(m)
                                if u < 7:
                                    high(u + 1, qt)
                                if u and qt == 3:
                                    attended(u - 1)
                        act.wait_ge(xy_used, i * 8 + 8)
                if kind == "attn":
                    l, lo = f, (0 if f == 0 else 1)
                    with act.Fori(0, 2) as i:
                        it, io = i + 2 * l, i + 2 * lo

                        def prep(s):
                            act.wait_ge(q_evac, it * 2 + (s + 1))
                            a.activation(qh[s][:], qf, ACT.Copy).then_inc(qh_done, 1)

                        def copy_pT(n):
                            act.wait_ge(pt_ready, it * 32 + (n + 1))
                            if n >= 2:
                                act.wait_ge(pv_done, it * 32 + (n - 1))
                            a.activation(pT[n % 2][:], bank(2 + n % 2, NCH * P)[0:CH, :], ACT.Copy
                                         ).then_inc(pt_done, 1)

                        def copy_oT(t):
                            act.wait_ge(ont_ready, io * 8 + (t + 1))
                            a.activation(oT, bank(6)[:, 0:P], ACT.Copy).then_inc(ot_done, 1)

                        prep(0)
                        for t in range(8 + 2):
                            if t == 2:
                                prep(1)
                            for gr in range(NG):
                                if 1 <= t < 9:
                                    copy_pT(4 * (t - 1) + gr)
                                if gr == 1 and t >= 2 and l != 1:
                                    copy_oT(t - 2)
                            if t < 8:
                                act.wait_ge(s_used, it * 32 + (CREDIT + 4 * t + 4))
                                a.activation(probs[t % 2][:, :, 0:GW], shifted[t % 2][:], ACT.Exp
                                             ).then_inc(p_ready, 1)
                        act.wait_ge(x_upd, it * 8 + 8)
                if kind == "ffn":
                    if f.route is not None:
                        act.wait_ge(lsub_ready, f.route + 1)
                        a.activation(lexp[:], lsub[:], ACT.Exp).then_inc(lexp_ready, 1)
                        for b in range(NB):
                            act.wait_ge(combT_ps, NB * f.route + b + 1)
                            a.activation(combT[:, b * 512:(b + 1) * 512], bank(4 + b)[0:NE, :], ACT.Copy
                                         ).then_inc(combT_done, 1)
                    if f.gated:
                        act.sem_inc(f.g_used, 2)
                    with act.Fori(0, f.iters) as i:
                        def func(k):
                            act.wait_ge(f.g_ready, i * f.NK + (k + 1))
                            if f.gated:
                                act.wait_ge(f.hf_done, i * f.NK + (k + 1))
                                ins = a.activation(act_out[k % 2][:], bank(k % 2), f.func)
                            else:
                                ins = a.activation(bank(k % 4), bank(k % 4), f.func)
                            ins.then_inc(f.g_used, 1)

                        def high(k):
                            if f.gated:
                                act.wait_ge(f.hf_done, i * f.NK + (k + 3))
                            else:
                                act.wait_ge(f.g_used, i * f.NK + (k + 1))
                            act.wait_ge(f.h_used, i * f.NK + (f.NK + k - 3))
                            a.activation(hh[k % 4], h_bank(f, k), ACT.Copy).then_inc(f.hh_done, 1)

                        for k in range(f.NK + 1):
                            if k < f.NK:
                                func(k)
                            if k >= 1:
                                high(k - 1)

        @block.vector
        def _(dve):
            v = nc.vector
            st = Steps(dve, dve_step)
            dve.wait_ge(small_loaded, 16 * 9)
            v.tensor_scalar(maskneg[:, 0], m0u, NEG, None, ALU.mult)
            st.link(v.tensor_scalar(m1f, m1i, 0.0, None, ALU.is_gt))
            v.tensor_reduce(seen[:], m1f, AX.X, ALU.min)
            for b in range(B):
                v.tensor_scalar(maskneg[:, 1, b * TB:(b + 1) * TB], bcast(m1f[:, b], TB, 1), NEG, None, ALU.mult)
            for b in range(B):
                ins = v.tensor_scalar(maskneg[:, 2, b * TB:(b + 1) * TB], m2u, -NEG, NEG, ALU.mult, ALU.add)
            st.link(ins)
            st.link(v.tensor_scalar(seen[:], seen[:], -1.0, 1.0, ALU.mult, ALU.add))
            st.link(v.reciprocal(rden[:, 0:B], seen[:]))
            v.tensor_tensor(seen[:], seen[:], rden[:, 0:B], ALU.mult).then_inc(mask_done, 1)
            dve.wait_ge(ctx_loaded, 32)
            dve.wait_ge(consts, 1)
            for l, c in enumerate((0, 2, None)):
                dve.wait_ge(k_ps, l + 1)
                if l:
                    dve.wait_ge(kl_done, l)
                if c is None:
                    ins = v.tensor_scalar(kf, bank(0, B * KC), HD ** -0.5, None, ALU.mult)
                else:
                    ins = v.tensor_scalar(kf, bank(0, B * KC), pcols[:, c + 1:c + 2], HD ** -0.5,
                                          ALU.add, ALU.mult)
                ins.then_inc(k_free, 1)
                dve.wait_ge(v_ps, l + 1)
                v.tensor_tensor(vall[:, l, :].rearrange("k (b d) -> k b d", b=B),
                                bank(1)[0:KC, :].rearrange("k (b d) -> k b d", b=B),
                                bcast(prows[0:KC, l, :], B, 1), ALU.add).then_inc(v_done, 1)
                dve.wait_ge(kh_done, l + 1)
                v.tensor_tensor(kl[:, l, :], kf, kh[:, l, :].bitcast(f32), ALU.subtract).then_inc(kl_done, 1)
            dve.wait_ge(wq_hi, 1)
            for l, c in enumerate((0, 4, 7)):
                ins = v.tensor_tensor(wql[:, l * P:(l + 1) * P], aw[:, c * P:(c + 1) * P],
                                      wqh[:, l * P:(l + 1) * P].bitcast(f32), ALU.subtract)
            ins.then_inc(wq_lo, 1)
            dve.wait_ge(small_loaded, 16 * 9)
            st.link(v.tensor_scalar(gwg[:], gw[:, 0, :], pcols[:, 4:5], None, ALU.mult))
            v.tensor_copy(gh[:, 0, :], gwg[:])
            st.link(v.tensor_copy(gh[:, 1:3, :], gw[:, 1:3, :]))
            v.tensor_tensor(gl[:, 0, :], gwg[:], gh[:, 0, :].bitcast(f32), ALU.subtract)
            st.link(v.tensor_tensor(gl[:, 1:3, :], gw[:, 1:3, :], gh[:, 1:3, :].bitcast(f32), ALU.subtract))
            st.link(v.memset(betaB[:], 1.0))
            v.tensor_scalar(betaB[:], betaB[:], pcols[:, 5:6], None, ALU.mult).then_inc(gate_ps, 1)

            def rsqrt(dst, var, scale=None, rows=slice(0, P)):
                if scale is not None:
                    st.link(v.tensor_tensor(vpe[rows, :], var, scale, ALU.mult))
                    st.link(v.tensor_tensor(vpe[rows, :], vpe[rows, :], scale, ALU.mult))
                    var = vpe[rows, :]
                st.link(v.tensor_scalar(vpe[rows, :], var, EPS, None, ALU.add))
                v.tensor_scalar(nhv[rows, :], vpe[rows, :], -0.5, None, ALU.mult)
                st.link(v.tensor_scalar(seed[rows, :], vpe[rows, :].bitcast(i32), 1, None, ALU.arith_shift_right))
                st.link(v.tensor_scalar(dst.bitcast(i32), seed[rows, :], -1.0, 1597463007.0, ALU.mult, ALU.add))
                for _ in range(3):
                    st.link(v.tensor_tensor(rtmp[rows, :], dst, dst, ALU.mult))
                    st.link(v.tensor_tensor(rtmp[rows, :], rtmp[rows, :], nhv[rows, :], ALU.mult))
                    st.link(v.scalar_tensor_tensor(dst, rtmp[rows, :], 1.5, dst, ALU.add, ALU.mult))

            def back_to_x(nth):
                for b in range(NB):
                    dve.wait_ge(yT_ps, NB * nth + b + 1)
                    xb = x[:, b * TB:(b + 1) * TB, :]
                    v.tensor_tensor(xb, xb, bank(6 + b % 2).rearrange("p (t d) -> p t d", d=D), ALU.add
                                    ).then_inc(x_added, 1)
                dve.wait_ge(x_added, NB * (nth + 1))
                dve.sem_inc(x_done, 1)

            KB = slice(0, KC)
            for b in range(B):
                ins = v.bn_stats(stats[KB, b, :], crow[:, b, :])
            st.link(ins)
            st.link(v.memset(mv[:], 1.0))
            for b in range(B):
                ins = v.bn_aggr(mv[KB, b, :], stats[KB, b, :])
            st.link(ins)
            rsqrt(rstd[KB, :], mv[KB, :, 1], rows=KB)
            for b in range(B):
                ins = v.tensor_scalar(crow[:, b, :], crow[:, b, :], mv[KB, b, 0:1], rstd[KB, b:b + 1],
                                      ALU.subtract, ALU.mult)
            ins.then_inc(med_ready, 1)
            st.link(v.memset(media[:].bitcast(f32), 0.0))
            st.link(v.tensor_scalar(xc[:, 0:LH], xc[:, 0:LH], LD ** -0.5, None, ALU.mult))
            dve.wait_ge(med_ps, 1)
            v.tensor_scalar(xg[0][:, 0:B * KC], bank(2, B * KC), xc[:, 3 * LH + 1:3 * LH + 2],
                            xc[:, 3 * LH + 2:3 * LH + 3], ALU.mult, ALU.add).then_inc(med_f, 1)
            dve.wait_ge(med_hi, 1)
            mid = [m.rearrange("p (b k) -> p b k", b=B)[:, :, 0:KC] for m in (mh, ml)]
            v.tensor_tensor(mid[1], xg[0][:, 0:B * KC].rearrange("p (b k) -> p b k", b=B), mid[0].bitcast(f32),
                            ALU.subtract).then_inc(med_lo, 1)
            dve.wait_ge(med_lo, 1)

            dve.wait_ge(x_loaded, 16)
            for n, (kind, f) in enumerate(phases):
                for t in range(NT):
                    ins = v.bn_stats(stats[:, t, :], x[:, t, :])
                st.link(ins)
                for t in range(NT):
                    ins = v.bn_aggr(mv[:, t, :], stats[:, t, :])
                st.link(ins)
                rsqrt(rstd[:], mv[:, :, 1])
                if kind == "wide":
                    rsqrt(rstd2[:], mv[:, :, 1], rstd[:])
                    st.link(v.tensor_tensor(rstd[:], rstd[:], rstd2[:], ALU.mult))
                for t in range(NT):
                    ins = v.tensor_scalar(xn[:, t, :], x[:, t, :], mv[:, t, 0:1], rstd[:, t:t + 1],
                                          ALU.subtract, ALU.mult)
                    if t % TB == TB - 1:
                        ins.then_inc(xn_ready, 1)
                for b in range(NB if kind == "wide" else 0):
                    dve.wait_ge(xT_ps, NB * n + b + 1)
                    if b >= 2:
                        dve.wait_ge(xl_done, NB * n + b - 1)
                    v.tensor_scalar(xg[b % 2], bank(b), xc[:, 3 * LH + 3:3 * LH + 4],
                                    xc[:, 3 * LH + 4:3 * LH + 5], ALU.mult, ALU.add).then_inc(xg_ready, 1)
                    dve.wait_ge(xh_done, NB * n + b + 1)
                    v.tensor_tensor(xl[:, b * 512:(b + 1) * 512], xg[b % 2],
                                    xh[:, b * 512:(b + 1) * 512].bitcast(f32), ALU.subtract).then_inc(xl_done, 1)
                for b in range(NB if kind != "wide" else 0):
                    dve.wait_ge(xh_done, NB * n + b + 1)
                    v.tensor_tensor(xl[:, b * 512:(b + 1) * 512], bank(b), xh[:, b * 512:(b + 1) * 512].bitcast(f32),
                                    ALU.subtract).then_inc(xl_done, 1)
                if kind == "attn":
                    l, lo = f, (0 if f == 0 else 1)
                    if l == 0:
                        dve.sem_inc(s_used, CREDIT)
                    for s in range(2):
                        st.link(v.memset(probs[s][:, :, GW:GWP], 0.0))
                    per = 8 * (4 + 1) + (8 if l == 1 else 0)
                    with dve.Fori(0, 2) as i:
                        st.enter(i, per)
                        it, io = i + 2 * l, i + 2 * lo

                        def prep(s):
                            dve.wait_ge(q_ps, it * 2 + (s + 1))
                            if s:
                                dve.wait_ge(q_ready, it * 2 + s)
                            if l < 2:
                                ins = v.tensor_scalar(qf, bank(7), pcols[:, 2 * l:2 * l + 1], None, ALU.add)
                            else:
                                ins = v.tensor_copy(qf, bank(7))
                            ins.then_inc(q_evac, 1)
                            dve.wait_ge(qh_done, it * 2 + (s + 1))
                            v.tensor_tensor(ql[s][:], qf, qh[s][:].bitcast(f32), ALU.subtract).then_inc(q_ready, 1)
                            dve.wait_ge(vx_ps, it * 2 + (s + 1))
                            v.tensor_tensor(
                                vx[s][:, :, :, 0:HD].rearrange("r j h d -> r (j h) d"),
                                bank(7)[0:CH, 0:NCH * D].rearrange("r (n d) -> r n d", d=HD),
                                bcast(cmask[:].rearrange("r j g h -> r (j g h)"), HD, 2),
                                ALU.mult).then_inc(vx_ready, 1)

                        def shift(n):
                            dve.wait_ge(s_ready, it * 32 + (CREDIT + n + 1))
                            s3 = bank(n % 2, GW).rearrange("p (h k) -> p h k", h=HG)
                            st.link(v.tensor_reduce(smax[:, n % 2, :], s3, AX.X, ALU.max))
                            v.tensor_tensor(shifted[(n // 4) % 2][:, n % 4, :].rearrange("p (h k) -> p h k", h=HG),
                                            s3, bcast(smax[:, n % 2, :], KC, 2), ALU.subtract).then_inc(s_used, 1)

                        def norm(t):
                            dve.wait_ge(pv_done, it * 32 + (4 * t + 4))
                            o3 = bank(4 + t % 2, H * VC).rearrange("p (h c) -> p h c", h=H)
                            st.link(v.reciprocal(rden[:], o3[:, :, HD:VC].rearrange("p h c -> p (h c)")))
                            if l == 1:
                                st.link(v.tensor_scalar(rden[:], rden[:], seen[:, ds(2 * i + (t // 4), 1)], None, ALU.mult))
                            if t >= 2 and l != 1:
                                dve.wait_ge(ont_ready, io * 8 + (t - 1))
                            ins = v.tensor_tensor(onorm[t % 2][:], o3[:, :, 0:HD], bcast(rden[:], HD, 2), ALU.mult)
                            ins.then_inc(o_used, 1)
                            if l == 1:
                                dve.wait_ge(o_used, it * 8 + (t + 1))
                                xt = x[:, ds(i * 8 + t, 1), :]
                                v.tensor_tensor(xt, xt, onorm[t % 2][:].rearrange("p h d -> p (h d)").unsqueeze(1),
                                                ALU.add).then_inc(x_upd, 1)

                        def update(t):
                            dve.wait_ge(out_ready, io * 8 + (t + 1))
                            xt = x[:, ds(i * 8 + t, 1), :]
                            v.tensor_tensor(xt, xt, bank(6)[:, P:2 * P].unsqueeze(1), ALU.add).then_inc(x_upd, 1)

                        prep(0)
                        for t in range(8 + 2):
                            if t == 2:
                                prep(1)
                            if t < 8:
                                if t >= 2:
                                    dve.wait_ge(p_ready, it * 8 + (t - 1))
                                for gr in range(NG):
                                    shift(4 * t + gr)
                            if 1 <= t < 9:
                                norm(t - 1)
                            if t >= 2 and l != 1:
                                update(t - 2)
                        dve.wait_ge(x_upd, it * 8 + 8)
                    st.leave(2)
                    dve.sem_inc(x_done, 1)
                elif kind == "wide":
                    st.link(v.memset(yacc, 0.0))
                    st.link(v.tensor_scalar(yacc, yacc, xc[:, 3 * LH:3 * LH + 1], None, ALU.add))
                    with dve.Fori(0, LH // 2) as i:
                        def part_low(u, part):
                            s, w = u % 2, i * 8 + u
                            dve.wait_ge(pj_hi, w * 4 + (part + 1))
                            add, sub = ALU.add, ALU.subtract
                            if part == 0:
                                ins = v.scalar_tensor_tensor(ql[s][:], bank(0), xc[:, ds(i * 2 + u // NB, 1)],
                                                             qh[s][:].bitcast(f32), add, sub)
                            elif part == 1:
                                ins = v.scalar_tensor_tensor(kxl[s][:, 0:S], bank(0),
                                                             xc[:, ds(i * 2 + (u // NB + LH), 1)],
                                                             kxh[s][:, 0:S].bitcast(f32), add, sub)
                            elif part == 2:
                                v.scalar_tensor_tensor(kxl[s][:, S:S + KP], bank(0, KP),
                                                       xc[:, ds(i * 2 + (u // NB + LH), 1)],
                                                       kxh[s][:, S:S + KP].bitcast(f32), add, sub)
                                ins = v.tensor_tensor(vxa[0:KC, s, 1, 512:640], bank(0)[0:KC, 128:256],
                                                      vxa[0:KC, s, 0, 512:640].bitcast(f32), sub)
                            else:
                                ins = v.tensor_tensor(vxa[:, s, 1, 0:512], bank(0),
                                                      vxa[:, s, 0, 0:512].bitcast(f32), sub)
                            ins.then_inc(pj_lo, 1)

                        def row_max(m):
                            dve.wait_ge(xs_ready, i * 32 + (m + 1))
                            v.tensor_reduce(xnm[:, m % XS:m % XS + 1], bank(2 + 2 * (m % 2), KEYS), AX.X, ALU.max,
                                            negate=True).then_inc(xs_max, 1)

                        def inverse(m):
                            dve.wait_ge(x_exp, i * 32 + (m + 1))
                            if m >= XS:
                                dve.wait_ge(xt_ready, i * 32 + (m - XS + 1))
                            z = slice(m % XS, m % XS + 1)
                            v.reciprocal(xrd[:, z], xsum[:, z]).then_inc(x_rec, 1)
                            dve.wait_ge(x_rec, i * 32 + (m + 1))
                            v.tensor_scalar(xdiag[m % XS], ident[:], xrd[:, z], None, ALU.mult).then_inc(x_norm, 1)

                        def turned_low(m):
                            u, qt = m // 4, m % 4
                            dve.wait_ge(xt_hi, i * 32 + (m + 1))
                            hi, lo = [xp4[u % 2][p].rearrange("p (j q) -> p j q", j=4)[:, :, qt * P:(qt + 1) * P]
                                      for p in range(2)]
                            v.tensor_tensor(lo, bank(6).rearrange("p (j q) -> p j q", j=4), hi.bitcast(f32),
                                            ALU.subtract)
                            hi, lo = [xp5[u % 2][p][0:KC, qt * P:(qt + 1) * P] for p in range(2)]
                            v.tensor_tensor(lo, bank(7)[0:KC, 0:P], hi.bitcast(f32), ALU.subtract
                                            ).then_inc(xt_lo, 1)

                        def attended_low(u):
                            dve.wait_ge(xo_hi, i * 8 + (u + 1))
                            v.scalar_tensor_tensor(oxl, bank(1), xc[:, ds(i * 2 + (u // NB + 2 * LH), 1)],
                                                   oxh.bitcast(f32), ALU.add, ALU.subtract).then_inc(xo_lo, 1)

                        def add_out(u):
                            dve.wait_ge(xy_ready, i * 8 + (8 + u + 1))
                            yb = yacc[:, (u % NB) * 512:(u % NB + 1) * 512]
                            if u:
                                dve.wait_ge(xy_used, i * 8 + u)
                            v.tensor_tensor(yb, yb, bank(1), ALU.add).then_inc(xy_used, 1)

                        for part in range(4):
                            part_low(0, part)
                        for u in range(8 + 2):
                            for qt in range(4):
                                m = 4 * u + qt
                                if m < 32:
                                    row_max(m)
                                if 1 <= m < 33:
                                    inverse(m - 1)
                                if 2 <= m < 34:
                                    turned_low(m - 2)
                                if u < 7:
                                    part_low(u + 1, qt)
                                if 1 <= u < 9 and qt == 3:
                                    attended_low(u - 1)
                                if u >= 2 and qt == 0:
                                    add_out(u - 2)
                        dve.wait_ge(xy_used, i * 8 + 8)
                    back_to_x(FF[6])
                else:
                    if f.route is not None:
                        if f.route == 0:
                            rsqrt(rstd2[:], mv[:, :, 1], rstd[:])
                        dve.wait_ge(lg_ps, f.route + 1)
                        lp = bank(4, NT * NE).rearrange("p (t e) -> p t e", e=NE)
                        if f.route == 0:
                            v.tensor_copy(gbias[:], bank(4)[:, 256:256 + NE])
                            st.link(v.tensor_tensor(logits[:], lp, bcast(rstd2[:], NE, 2), ALU.mult))
                            st.link(v.tensor_tensor(logits[:], logits[:], bcast(gbias[:], NT, 1), ALU.add))
                        else:
                            st.link(v.tensor_copy(logits[:], lp))
                        st.link(v.tensor_reduce(lmax[:], logits[:], AX.X, ALU.max))
                        v.tensor_tensor(lsub[:], logits[:], bcast(lmax[:], NE, 2), ALU.subtract).then_inc(lsub_ready, 1)
                        mine, other = bcast(logits[:], NE, 3), bcast(logits[:], NE, 2)
                        st.link(v.tensor_tensor(tied[:], other, mine, ALU.is_equal))
                        st.link(v.tensor_tensor(tied[:], tied[:], bcast(tri[:], NT, 1), ALU.mult))
                        st.link(v.tensor_tensor(above[:], other, mine, ALU.is_gt))
                        st.link(v.tensor_tensor(above[:], above[:], tied[:], ALU.add))
                        st.link(v.tensor_reduce(rank[:], above[:], AX.X, ALU.add))
                        st.link(v.tensor_scalar(rank[:], rank[:], 2.0, None, ALU.is_lt))
                        dve.wait_ge(lexp_ready, f.route + 1)
                        st.link(v.tensor_tensor(comb[:], lexp[:], rank[:], ALU.mult))
                        st.link(v.tensor_reduce(wsum[:], (lexp if f.route == 0 else comb)[:], AX.X, ALU.add))
                        st.link(v.reciprocal(wsum[:], wsum[:]))
                        v.tensor_tensor(comb[:], comb[:], bcast(wsum[:], NE, 2), ALU.mult).then_inc(comb_ready, 1)
                    if f.gated:
                        dve.sem_inc(f.hf_done, 2)
                    dve.sem_inc(f.h_ready, 4)
                    dve.sem_inc(f.y_used, f.NS)
                    if f.route is not None:
                        dve.wait_ge(comb_stored, 32 * (f.route + 1))
                    st.link(v.memset(yacc, 0.0))
                    with dve.Fori(0, f.iters) as i:
                        st.enter(i, f.NS if f.route is not None else 0)

                        def low(k):
                            if f.gated:
                                dve.wait_ge(f.g_used, i * f.NK + (k + 3))
                                dve.wait_ge(f.u_ready, i * f.NK + (k + 1))
                                v.tensor_tensor(h_bank(f, k), act_out[k % 2][:], h_bank(f, k), ALU.mult
                                                ).then_inc(f.hf_done, 1)

                        def finish_low(k):
                            dve.wait_ge(f.hh_done, i * f.NK + (k + 1))
                            ins = v.tensor_tensor(hl[k % 4], h_bank(f, k), hh[k % 4].bitcast(f32), ALU.subtract)
                            ins.then_inc(f.h_ready, 1)

                        def result(s):
                            dve.wait_ge(f.h_used, i * f.NK + (f.NK + (s + 1) * f.nf))
                            if s:
                                dve.wait_ge(f.y_used, i * f.NS + (f.NS + s))
                            e, b = s // NB, s % NB
                            sl = slice(b * 512, (b + 1) * 512)
                            y = bank(4 + s % 2)
                            if f.route is not None:
                                if b == 0:
                                    dve.wait_ge(f.cb_in[e], i * 16 + 16)
                                st.link(v.tensor_tensor(y, y, combs[e][:, sl], ALU.mult))
                            v.tensor_tensor(yacc[:, sl], yacc[:, sl], y, ALU.add).then_inc(f.y_used, 1)

                        done = 0
                        for k in range(f.NK + 1):
                            if k < f.NK:
                                low(k)
                            if k >= 1:
                                finish_low(k - 1)
                            if k > f.nf * (done + 1) + LAG:
                                result(done)
                                done += 1
                        while done < f.NS:
                            result(done)
                            done += 1
                        dve.wait_ge(f.y_used, i * f.NS + 2 * f.NS)
                    st.leave(f.iters)
                    back_to_x(FF[f.index])

        @block.tensor
        def _(pe):
            mm = nc.tensor.matmul

            def mm3(dst, lh, ll, rh, rl, start=True, stop=True):
                mm(dst, ll, rh, start=start, stop=False)
                mm(dst, lh, rl, start=False, stop=False)
                return mm(dst, lh, rh, start=False, stop=stop)

            pe.wait_ge(ctx_loaded, 32)
            for l, (ck, cv) in enumerate(((1, 2), (5, 6), (8, 9))):
                if l:
                    pe.wait_ge(k_free, l)
                mm(bank(0, B * KC), aw[:, ck * P:(ck + 1) * P], ctxT[:], start=True, stop=True).then_inc(k_ps, 1)
                if l:
                    pe.wait_ge(v_done, l)
                for b in range(B):
                    ins = mm(bank(1)[0:KC, b * D:(b + 1) * D], ctxT[:, b * KC:(b + 1) * KC],
                             aw[:, cv * P:(cv + 1) * P], start=True, stop=True)
                ins.then_inc(v_ps, 1)
            pe.wait_ge(k_free, 3)
            pe.wait_ge(v_done, 3)
            pe.wait_ge(consts, 1)
            pe.wait_ge(med_ready, 1)
            for b in range(B):
                ins = nc.tensor.transpose(bank(2)[:, b * KC:(b + 1) * KC], crow[:, b, :], ident[0:KC, 0:KC])
            ins.then_inc(med_ps, 1)
            pe.wait_ge(med_lo, 1)

            def yacc_back(nth, ready):
                for b in range(NB):
                    ready(b)
                    if b >= 2:
                        pe.wait_ge(x_added, NB * nth + b - 1)
                    for t in range(TB):
                        ins = nc.tensor.transpose(bank(6 + b % 2)[:, t * P:(t + 1) * P],
                                                  yacc[:, (b * TB + t) * P:(b * TB + t + 1) * P], ident[:])
                    ins.then_inc(yT_ps, 1)

            for n, (kind, f) in enumerate(phases):
                for b in range(NB):
                    pe.wait_ge(xn_ready, NB * n + b + 1)
                    for t in range(TB):
                        ins = nc.tensor.transpose(bank(b)[:, t * P:(t + 1) * P], xn[:, b * TB + t, :], ident[:])
                    ins.then_inc(xT_ps, 1)
                if kind == "attn":
                    l, lo = f, (0 if f == 0 else 1)
                    if l == 0:
                        pe.sem_inc(s_ready, CREDIT)
                        pe.wait_ge(wq_lo, 1)
                        pe.wait_ge(mask_done, 1)
                    pe.wait_ge(xl_done, NB * (n + 1))
                    with pe.Fori(0, 2) as i:
                        it, io = i + 2 * l, i + 2 * lo

                        def prep(s):
                            if s:
                                pe.wait_ge(vx_ready, it * 2 + s)
                            cur = ds(i * 1024 + s * 512, 512)
                            w = slice(l * P, (l + 1) * P)
                            mm3(bank(7), wqh[:, w], wql[:, w], xh[:, cur], xl[:, cur]).then_inc(q_ps, 1)
                            pe.wait_ge(q_evac, it * 2 + (s + 1))
                            for j in range(NCH):
                                ins = mm(bank(7)[0:CH, j * D:(j + 1) * D], spreadp[:, j * CH:(j + 1) * CH],
                                         vall[:, l, ds(i * 2 * D + s * D, D)], start=True, stop=True)
                            ins.then_inc(vx_ps, 1)

                        def scores(n):
                            t, gr = n // 4, n % 4
                            s, tq = t // 4, t % 4
                            if tq == 0 and gr == 0:
                                pe.wait_ge(q_ready, it * 2 + (s + 1))
                                pe.wait_ge(kb_ready, it * 2 + (s + 1))
                            pe.wait_ge(s_used, it * 32 + (CREDIT + n - 1))
                            q = slice(tq * P, (tq + 1) * P)
                            w = slice(gr * GW, (gr + 1) * GW)
                            dst = bank(n % 2, GW)
                            mm3(dst, qh[s][:, q], ql[s][:, q], kbh[s][:, w], kbl[s][:, w], stop=False)
                            mm(dst.rearrange("p (h k) -> p h k", h=HG), identb[:],
                               maskneg[:, l, ds(i * 8 + t, 1), :].broadcast_to([P, HG, KC]),
                               start=False, stop=True).then_inc(s_ready, 1)

                        def transp(n):
                            t, gr = n // 4, n % 4
                            if gr == 0:
                                pe.wait_ge(p_ready, it * 8 + (t + 1))
                            if n >= 2:
                                pe.wait_ge(pt_done, it * 32 + (n - 1))
                            for j in range(NCH):
                                ins = nc.tensor.transpose(bank(2 + n % 2)[0:CH, j * P:(j + 1) * P],
                                                          probs[t % 2][:, gr, j * CH:(j + 1) * CH], ident[:])
                            ins.then_inc(pt_ready, 1)

                        def values(n):
                            t, gr = n // 4, n % 4
                            if t % 4 == 0 and gr == 0:
                                pe.wait_ge(vx_ready, it * 2 + (t // 4 + 1))
                            if gr == 0 and t >= 2:
                                pe.wait_ge(o_used, it * 8 + (t - 1))
                            pe.wait_ge(pt_done, it * 32 + (n + 1))
                            for j in range(NCH):
                                ins = mm(bank(4 + t % 2)[:, gr * HG * VC:(gr + 1) * HG * VC],
                                         pT[n % 2][:, j * P:(j + 1) * P],
                                         vx[t // 4][:, j, gr * HG:(gr + 1) * HG, :].rearrange("r h c -> r (h c)"),
                                         start=(j == 0), stop=(j == NCH - 1))
                            ins.then_inc(pv_done, 1)

                        def turn(t):
                            pe.wait_ge(o_used, it * 8 + (t + 1))
                            if t >= 1:
                                pe.wait_ge(x_upd, it * 8 + t)
                            nc.tensor.transpose(bank(6)[:, 0:P], onorm[t % 2][:].rearrange("p h d -> p (h d)"),
                                                ident[:]).then_inc(ont_ready, 1)

                        def project(t):
                            pe.wait_ge(ot_done, io * 8 + (t + 1))
                            wo = aw[:, (3 if l == 0 else 10) * P:(4 if l == 0 else 11) * P]
                            ins = mm(bank(6)[:, P:2 * P], oT, wo, start=True, stop=(l != 0))
                            if l == 0:
                                ins = mm(bank(6)[:, P:2 * P], ones_row[:], worow[:], start=False, stop=True)
                            ins.then_inc(out_ready, 1)

                        prep(0)
                        for t in range(8 + 2):
                            if t == 2:
                                prep(1)
                            for gr in range(NG):
                                if t < 8:
                                    scores(4 * t + gr)
                                if 1 <= t < 9:
                                    transp(4 * (t - 1) + gr)
                                    if gr:
                                        values(4 * (t - 1) + gr - 1)
                                if gr == 1 and t >= 2 and l != 1:
                                    turn(t - 2)
                            if 1 <= t < 9:
                                values(4 * (t - 1) + 3)
                            if t >= 2 and l != 1:
                                project(t - 2)
                        pe.wait_ge(x_upd, it * 8 + 8)
                elif kind == "wide":
                    pe.wait_ge(xl_done, NB * (n + 1))
                    pe.sem_inc(xy_ready, 8)
                    with pe.Fori(0, LH // 2) as i:
                        def wt(u, c):
                            o = (u // NB) * 512 + c * P
                            return wh[:, o:o + P], wl[:, o:o + P]

                        def project(u, part):
                            s, b, w = u % 2, u % NB, i * 8 + u
                            tk = slice(b * S, (b + 1) * S)
                            md = slice(b * KP, (b + 1) * KP)
                            if part == 0 and u % NB == 0:
                                pe.wait_ge(x_split, i * 2 + (2 + u // NB + 1))
                            if part or u:
                                pe.wait_ge(pj_lo, w * 4 + part)
                            if part == 0:
                                ins = mm3(bank(0), *wt(u, 0), xh[:, tk], xl[:, tk])
                            elif part == 1:
                                ins = mm3(bank(0), *wt(u, 1), xh[:, tk], xl[:, tk])
                            elif part == 2:
                                mm3(bank(0, KP), *wt(u, 1), mh[:, md], ml[:, md])
                                mc = slice(b * KP, b * KP + KC)
                                ins = mm3(bank(0)[0:KC, 128:256], mh[:, mc], ml[:, mc], *wt(u, 2))
                            else:
                                for t in range(TB):
                                    tt = slice(b * S + t * P, b * S + (t + 1) * P)
                                    ins = mm3(bank(0)[:, t * P:(t + 1) * P], xh[:, tt], xl[:, tt], *wt(u, 2))
                            ins.then_inc(pj_ps, 1)

                        def scores(m):
                            u, qt = m // 4, m % 4
                            s = u % 2
                            if qt == 0:
                                pe.wait_ge(pj_lo, i * 32 + (u + 1) * 4)
                            if m >= 2:
                                pe.wait_ge(x_exp, i * 32 + (m - 1))
                            q = slice(qt * P, (qt + 1) * P)
                            for c, w in ((0, S), (1, KP)):
                                kk = slice(c * S, c * S + w)
                                ins = mm3(bank(2 + 2 * (m % 2) + c, w), qh[s][:, q], ql[s][:, q],
                                          kxh[s][:, kk], kxl[s][:, kk])
                            ins.then_inc(xs_ready, 1)

                        def turn(m):
                            pe.wait_ge(x_norm, i * 32 + (m + 1))
                            if m:
                                pe.wait_ge(xt_lo, i * 32 + m)
                            for j in range(4):
                                mm(bank(6)[:, j * P:(j + 1) * P], xprob[m % XS][:, j * P:(j + 1) * P], xdiag[m % XS],
                                   start=True, stop=True)
                            mm(bank(7)[0:KC, 0:P], xprob[m % XS][:, S:KEYS], xdiag[m % XS], start=True, stop=True
                               ).then_inc(xt_ready, 1)

                        def attend(u, chunks):
                            s = u % 2
                            if chunks[0] == 4:
                                pe.wait_ge(xt_lo, i * 32 + (4 * u + 4))
                                if u:
                                    pe.wait_ge(xy_used, i * 8 + u)
                            for j in chunks:
                                vh, vl = [vxa[0:P if j < 4 else KC, s, p, j * P:(j + 1) * P] for p in range(2)]
                                ph, pl = [xp4[s][p][:, j * S:(j + 1) * S] if j < 4 else xp5[s][p][0:KC, :]
                                          for p in range(2)]
                                ins = mm3(bank(1), vh, vl, ph, pl, start=(j == 4), stop=(j == 3))
                            if chunks[-1] == 3:
                                ins.then_inc(xo_ready, 1)

                        def out_product(u):
                            pe.wait_ge(xo_lo, i * 8 + (u + 1))
                            mm3(bank(1), *wt(u, 3), oxh, oxl).then_inc(xy_ready, 1)

                        for part in range(4):
                            project(0, part)
                        for u in range(8 + 2):
                            for qt in range(4):
                                m = 4 * u + qt
                                if m < 32:
                                    scores(m)
                                if 2 <= m < 34:
                                    turn(m - 2)
                                if 1 <= u < 9 and qt == 2:
                                    attend(u - 1, (4, 0))
                                if 1 <= u < 9 and qt == 3:
                                    attend(u - 1, (1, 2, 3))
                                if u < 7:
                                    project(u + 1, qt)
                                if u >= 2 and qt == 0:
                                    out_product(u - 2)
                        pe.wait_ge(xy_used, i * 8 + 8)
                    yacc_back(FF[6], lambda b: None)
                else:
                    pe.wait_ge(xl_done, NB * (n + 1))
                    if f.route is not None:
                        pe.wait_ge(gate_ps, 1)
                        r = f.route
                        for t in range(NT):
                            tk = slice(t * P, (t + 1) * P)
                            ins = mm3(bank(4)[:, t * NE:(t + 1) * NE], xh[:, tk], xl[:, tk], gh[:, r, :], gl[:, r, :])
                        if r == 0:
                            ins = mm(bank(4)[:, 256:256 + NE], betaB[:], gw[:, 0, :], start=True, stop=True)
                        ins.then_inc(lg_ps, 1)
                        pe.wait_ge(comb_ready, r + 1)
                        for b in range(NB):
                            for t in range(TB):
                                ins = nc.tensor.transpose(bank(4 + b)[0:NE, t * P:(t + 1) * P],
                                                          comb[:, b * TB + t, :], ident[:])
                            ins.then_inc(combT_ps, 1)
                        pe.wait_ge(combT_done, NB * (r + 1))
                    pe.sem_inc(f.h_used, f.NK)
                    with pe.Fori(0, f.iters) as i:
                        def up(k):
                            s, c = k // f.nf, k % f.nf
                            e, b = s // NB, s % NB
                            if b == 0 and c == 0:
                                pe.wait_ge(f.split, i * f.U + (f.U + e + 1))
                            tk = slice(b * 512, (b + 1) * 512)
                            w = slice(e * f.wc + c * P, e * f.wc + (c + 1) * P)
                            if f.gated:
                                pe.wait_ge(f.g_used, i * f.NK + (k + 1))
                            else:
                                pe.wait_ge(f.h_ready, i * f.NK + (k + 1))
                            mm3(bank(k % 2 if f.gated else k % 4), wh[:, w], wl[:, w], xh[:, tk], xl[:, tk]).then_inc(f.g_ready, 1)
                            if f.gated:
                                w = slice(w.start + f.nf * P, w.stop + f.nf * P)
                                pe.wait_ge(f.h_ready, i * f.NK + (k + 1))
                                mm3(bank(H_BANKS[k % 4]), wh[:, w], wl[:, w], xh[:, tk], xl[:, tk]).then_inc(f.u_ready, 1)

                        def down(k):
                            s, c = k // f.nf, k % f.nf
                            e = s // NB
                            o = e * f.wc + (2 if f.gated else 1) * f.nf * P + c * P
                            if c == 0:
                                pe.wait_ge(f.y_used, i * f.NS + (f.NS + s - 1))
                            pe.wait_ge(f.h_ready, i * f.NK + (k + 5))
                            dst = bank(4 + s % 2)
                            mm(dst, wl[:, o:o + P], hh[k % 4], start=(c == 0), stop=False)
                            mm(dst, wh[:, o:o + P], hl[k % 4], start=False, stop=False)
                            ins = mm(dst, wh[:, o:o + P], hh[k % 4], start=False, stop=(c == f.nf - 1))
                            ins.then_inc(f.h_used, 1)

                        for k in range(f.NK + LAG):
                            if k < f.NK:
                                up(k)
                            if k >= LAG:
                                down(k - LAG)
                    yacc_back(FF[f.index],
                              lambda b: pe.wait_ge(f.y_used, f.NS * (f.iters + 1) - (NB - 1 - b)))


_OUTS = [((4, 512, 128), 'float32')]


def kernel(**inputs):
    import numpy as _np
    import concourse.bacc as _bacc
    from concourse import mybir as _mybir
    from concourse.bass_utils import run_bass_kernel_spmd as _run

    g = {k: _np.asarray(v) for k, v in inputs.items()}

    def chunked(w):
        e, f, d = w.shape
        return w.reshape(e, f // 128, 128, d).transpose(0, 2, 1, 3).reshape(e, 128, -1)

    def heads(w):
        return w.reshape(128, 8, 128).transpose(1, 0, 2)

    cat = _np.concatenate
    packed = {
        "x": g["x"],
        "ctx_t": g["ctx_1024"].reshape(-1, 128).T,
        "ctx_rows": g["ctx_1024"],
        "mask0": g["mask_Bx1xSxS2_bk1"],
        "mask1": g["mask_BxS2_ik0"],
        "mask2": g["mask_1x1xSxS2_bk0"],
        "attn_w": cat([g["L0_xattn_Wq"], g["L0_xattn_Wk"], g["L0_xattn_Wv"], g["L0_xattn_Wo"],
                       g["L1_xattn_q_w"].T, g["L1_xattn_k_w"].T, g["L1_xattn_v_w"].T,
                       g["L2_xattn_Wq"].T, g["L2_xattn_Wk"].T, g["L2_xattn_Wv"].T, g["L2_xattn_Wo"].T], axis=1),
        "cols": _np.stack([g["L0_xattn_bq"], g["L0_xattn_bk"], g["L1_xattn_q_b"], g["L1_xattn_k_b"],
                           g["L0_ffn_ln_gamma"], g["L0_ffn_ln_beta"], g["L0_ffn_ln_gamma"],
                           g["L0_ffn_ln_beta"]], axis=1),
        "rows": _np.stack([g["L0_xattn_bv"], g["L1_xattn_v_b"], g["L0_xattn_bo"]]),
        "gates": cat([g["L0_ffn_gate_w"].T, g["L2_ffn_w_router"], g["L3_ffn_gate_w"]], axis=1),
        "f0": cat([g["L0_ffn_w1"].transpose(0, 2, 1), chunked(g["L0_ffn_w2"].transpose(0, 2, 1))], axis=2),
        "f1": cat([g["L1_ffn_Wg"], g["L1_ffn_Wu"], chunked(g["L1_ffn_Wd"])], axis=2),
        "f2": cat([cat([g["L2_ffn_w1_routed"], g["L2_ffn_w1_shared"][None]], axis=0),
                   chunked(cat([g["L2_ffn_w2_routed"], g["L2_ffn_w2_shared"][None]], axis=0))], axis=2),
        "f3": cat([g["L3_ffn_w1"], g["L3_ffn_w3"], chunked(g["L3_ffn_w2"])], axis=2),
        "xw": cat([heads(g["L3_xattn_Wq"]), heads(g["L3_xattn_Wkv"][:, :1024]), heads(g["L3_xattn_Wkv"][:, 1024:]),
                   g["L3_xattn_Wo"].reshape(8, 128, 128)], axis=2),
        "xcols": cat([g["L3_xattn_bq"].reshape(8, 128), g["L3_xattn_bkv"].reshape(16, 128),
                      g["L3_xattn_bo"][None], g["L3_xattn_gamma_media"][None], g["L3_xattn_beta_media"][None],
                      g["L3_xattn_gamma_lat"][None], g["L3_xattn_beta_lat"][None]], axis=0).T,
    }
    nc = _bacc.Bacc("TRN2", target_bir_lowering=False, num_devices=1)
    arrays, args = {}, []
    for name, a in packed.items():
        a = _np.ascontiguousarray(a)
        arrays[f"in_{name}_dram"] = a
        args.append(nc.dram_tensor(f"in_{name}_dram", a.shape, _mybir.dt.from_np(a.dtype), kind="ExternalInput").ap())
    for i, (shape, dtype) in enumerate(_OUTS):
        dt = _mybir.dt.from_np(_np.dtype(dtype))
        args.append(nc.dram_tensor(f"out_{i}_dram", shape, dt, kind="ExternalOutput").ap())
    build(nc, *args)
    r = _run(nc, [arrays], core_ids=[0])
    return r.results[0]["out_0_dram"]
```

```python
import concourse.bass as bass
from concourse import mybir
from contextlib import ExitStack

PHASES = 8

B, S, D = 4, 512, 128
KC = 77
P = 128
NT = B * S // P
TB = 4
NB = NT // TB
EPS = 1e-5
NE = 8
H, HD = 16, 8
HG = 4
NG = H // HG
GW = HG * KC
NCH = 3
CH = -(-GW // NCH)
GWP = NCH * CH
VC = HD + 1
NEG = -1e30
LH, LD = 8, 128
KEYS = S + KC
KP = KC + 1
HB = 4
UB = HB * NB
XS = 4
CREDIT = 4096


class Experts:
    pass


def build(nc, x_in, ctx_t, ctx_rows, mask0, mask1, mask2, attn_w, cols, rows, gates,
          f0, f1, f2, f3, xw, xcols, out):
    f32, f32r, bf16 = mybir.dt.float32, mybir.dt.float32r, mybir.dt.bfloat16
    i32, u8 = mybir.dt.int32, mybir.dt.uint8
    ALU = mybir.AluOpType
    ACT = mybir.ActivationFunctionType
    AX = mybir.AxisListType
    ds = bass.ds

    stack = ExitStack()
    with stack:
        def sb(name, shape, dt=f32):
            return stack.enter_context(nc.sbuf_tensor(name, shape, dt))

        def sem(name):
            return stack.enter_context(nc.semaphore(name))

        psum = stack.enter_context(nc.psum_tensor("psum", [P, 8 * 512], f32))

        def bank(n, width=512):
            return psum[:, n * 512:n * 512 + width]

        x = sb("x", [P, NT, D])
        xh = sb("xh", [P, NT * P], f32r)
        xl = sb("xl", [P, NT * P], f32r)
        xn = sb("xn", [P, NT, D])
        ident = sb("ident", [P, P])
        identb = sb("identb", [P, P], bf16)
        ones_row = sb("ones_row", [1, P])
        stats = sb("stats", [P, NT, 6])
        mv = sb("mv", [P, NT, 2])
        vpe = sb("vpe", [P, NT])
        nhv = sb("nhv", [P, NT])
        seed = sb("seed", [P, NT], i32)
        rstd = sb("rstd", [P, NT])
        rtmp = sb("rtmp", [P, NT])
        rstd2 = sb("rstd2", [P, NT])
        ctxT = sb("ctxT", [P, B * KC])
        aw = sb("aw", [P, 11 * P])
        wqh = sb("wqh", [P, 3 * P], f32r)
        wql = sb("wql", [P, 3 * P], f32r)
        pcols = sb("pcols", [P, 8])
        prows = sb("prows", [P, 3, D])
        worow = sb("worow", [1, D])
        kh = sb("kh", [P, 3, B * KC], f32r)
        kl = sb("kl", [P, 3, B * KC], f32r)
        vall = sb("vall", [KC, 3, B * D])
        hmask = sb("hmask", [P, H])
        cmask = sb("cmask", [CH, NCH, NG, HG])
        spreadp = sb("spreadp", [KC, GWP])
        spread = spreadp[:, 0:GW].rearrange("k (h c) -> k h c", h=HG)
        kb = sb("kb", [P, 4 * H * KC], f32r)
        kbh = [kb[:, s * H * KC:(s + 1) * H * KC] for s in range(2)]
        kbl = [kb[:, (2 + s) * H * KC:(3 + s) * H * KC] for s in range(2)]
        vx = [sb(f"vx{s}", [CH, NCH, H, VC]) for s in range(2)]
        qh = [sb(f"qh{s}", [P, S], f32r) for s in range(2)]
        ql = [sb(f"ql{s}", [P, S], f32r) for s in range(2)]
        maskneg = sb("maskneg", [P, 3, NT, KC], bf16)
        seen = sb("seen", [P, B])
        smax = sb("smax", [P, 2, HG])
        shared = sb("shared", [P, 3 * NT * P])
        m0u = shared[:, 0:NT * KC // 4].bitcast(u8).rearrange("p (t k) -> p t k", k=KC)
        m1i = shared[:, 512:512 + B * KC].bitcast(i32).rearrange("p (b k) -> p b k", k=KC)
        m1f = shared[:, 1024:1024 + B * KC].rearrange("p (b k) -> p b k", k=KC)
        m2u = shared[:, 1536:1536 + TB * KC // 4].bitcast(u8).rearrange("p (t k) -> p t k", k=KC)
        shifted = [shared[:, s * NG * GW:(s + 1) * NG * GW].rearrange("p (g k) -> p g k", g=NG)
                   for s in range(2)]
        probs = [shared[:, 2 * NG * GW + s * NG * GWP:2 * NG * GW + (s + 1) * NG * GWP]
                 .rearrange("p (g k) -> p g k", g=NG) for s in range(2)]
        pT = [sb(f"pT{s}", [CH, NCH * P]) for s in range(2)]
        rden = sb("rden", [P, H])
        onorm = [sb(f"onorm{s}", [P, H, HD]) for s in range(2)]
        wraw = sb("wraw", [P, 3072])
        kf = wraw[:, 2560:2560 + B * KC]
        wh = sb("wh", [P, 3072], f32r)
        wl = sb("wl", [P, 3072], f32r)
        act_out = [sb(f"act_out{s}", [P, 512]) for s in range(2)]
        qf = act_out[0][:, :]
        oT = sb("oT", [P, P])[:, :]
        hhl = sb("hhl", [P, 8 * 512], f32r)
        hh = [hhl[:, s * 512:(s + 1) * 512] for s in range(4)]
        hl = [hhl[:, (4 + s) * 512:(5 + s) * 512] for s in range(4)]
        yacc = xn[:, :, :].rearrange("p t d -> p (t d)")
        combs = [shared[:, s * NT * P:(s + 1) * NT * P] for s in range(3)]
        gw = sb("gw", [P, 3, NE])
        gwg = sb("gwg", [P, NE])
        ghl = sb("ghl", [P, 3, 2 * NE], f32r)
        gh, gl = ghl[:, :, 0:NE], ghl[:, :, NE:2 * NE]
        betaB = sb("betaB", [P, P])
        gbias = sb("gbias", [P, NE])
        logits = sb("logits", [P, NT, NE])
        lmax = sb("lmax", [P, NT])
        lsub = sb("lsub", [P, NT, NE])
        lexp = sb("lexp", [P, NT, NE])
        tri = sb("tri", [P, NE, NE], bf16)
        above = shared[:, 2048:2048 + NT * NE * NE // 2].bitcast(bf16).rearrange("p (t a b) -> p t a b", a=NE, b=NE)
        tied = shared[:, 3072:3072 + NT * NE * NE // 2].bitcast(bf16).rearrange("p (t a b) -> p t a b", a=NE, b=NE)
        rank = sb("rank", [P, NT, NE])
        xc = sb("xc", [P, 3 * LH + 5])
        xcur = sb("xcur", [P, 3, HB])
        crow = wraw[0:KC, 2048:2048 + B * D].rearrange("k (b d) -> k b d", b=B)
        media = sb("media", [P, 2, B * KP], f32r)
        med_full = shared[:, 2 * NT * P:2 * NT * P + B * KC]
        mh, ml = media[:, 0, :], media[:, 1, :]
        tails = [wl[:, 1024 + n * 512:1024 + (n + 1) * 512] for n in range(4)]
        xp4 = [[kb[:, 0:2048], kb[:, 2048:4096]], [hhl[:, 0:2048], hhl[:, 2048:4096]]]
        xp5 = [[kb[:, 4096:4608], tails[0]], [tails[1], tails[2]]]
        kxh = [wh[:, 1024 + s * 640:1024 + s * 640 + S + KP] for s in range(2)]
        kxl = [wh[:, 1024 + 2 * 640:1024 + 2 * 640 + S + KP], sb("kxl1", [P, S + KP], f32r)[:]]
        vxa = sb("vxa", [P, 2, 2, 5 * P], f32r)
        xsum = sb("xsum", [P, XS])
        xnm = sb("xnm", [P, XS])
        xrd = sb("xrd", [P, XS])
        xprob = [shared[:, s * 640:s * 640 + KEYS] for s in range(XS)]
        xdiag = [shared[:, XS * 640 + s * P:XS * 640 + (s + 1) * P] for s in range(XS)]
        xg = [shared[:, XS * 768 + s * 512:XS * 768 + (s + 1) * 512] for s in range(2)]
        oxh, oxl = [k[:, :, :].rearrange("p l k -> p (l k)")[:, 0:S] for k in (kh, kl)]
        wsum = sb("wsum", [P, NT])
        comb = sb("comb", [P, NT, NE])
        combT = shared[0:NE, 0:NT * P]
        one_rows = sb("one_rows", [NT, P])
        comb_dram = [nc.dram_tensor(f"comb_dram{n}", [NE + 1, NT * P], f32, kind="Internal").ap() for n in range(3)]

        x_loaded, ctx_loaded, small_loaded = sem("x_loaded"), sem("ctx_loaded"), sem("small_loaded")
        mask_loaded, late_loaded = sem("mask_loaded"), sem("late_loaded")
        out_stored = sem("out_stored")
        consts = sem("consts")
        dve_step, act_step, pool_step = sem("dve_step"), sem("act_step"), sem("pool_step")
        xn_ready, xT_ps, xh_done, xl_done = sem("xn_ready"), sem("xT_ps"), sem("xh_done"), sem("xl_done")
        x_done = sem("x_done")
        k_ps, k_free, kh_done, kl_done = sem("k_ps"), sem("k_free"), sem("kh_done"), sem("kl_done")
        v_ps, v_done = sem("v_ps"), sem("v_done")
        wq_hi, wq_lo = sem("wq_hi"), sem("wq_lo")
        mask_done = sem("mask_done")
        q_ps, q_evac, qh_done, q_ready = sem("q_ps"), sem("q_evac"), sem("qh_done"), sem("q_ready")
        vx_ps, vx_ready, kb_ready = sem("vx_ps"), sem("vx_ready"), sem("kb_ready")
        s_ready, s_used, p_ready = sem("s_ready"), sem("s_used"), sem("p_ready")
        pt_ready, pt_done, pv_done = sem("pt_ready"), sem("pt_done"), sem("pv_done")
        o_used, ont_ready, ot_done, out_ready, x_upd = (
            sem("o_used"), sem("ont_ready"), sem("ot_done"), sem("out_ready"), sem("x_upd"))
        lg_ps, lsub_ready, lexp_ready, comb_ready, combT_ps, combT_done, comb_stored, gate_done = (
            sem("lg_ps"), sem("lsub_ready"), sem("lexp_ready"), sem("comb_ready"), sem("combT_ps"),
            sem("combT_done"), sem("comb_stored"), sem("gate_done"))
        xg_ready, med_ready, med_ps, med_hi, med_lo, med_f = (
            sem("xg_ready"), sem("med_ready"), sem("med_ps"), sem("med_hi"), sem("med_lo"), sem("med_f"))
        x_split, x_split_hi, x_scaled = sem("x_split"), sem("x_split_hi"), sem("x_scaled")
        xw_in = [sem(f"xw_in{s}") for s in range(2)]
        pj_ps, pj_hi, pj_lo = sem("pj_ps"), sem("pj_hi"), sem("pj_lo")
        xs_ready, xs_max, x_exp, x_rec, x_norm = (
            sem("xs_ready"), sem("xs_max"), sem("x_exp"), sem("x_rec"), sem("x_norm"))
        xt_ready, xt_hi, xt_lo = sem("xt_ready"), sem("xt_hi"), sem("xt_lo")
        xo_ready, xo_hi, xo_lo, xy_ready, xy_used = (
            sem("xo_ready"), sem("xo_hi"), sem("xo_lo"), sem("xy_ready"), sem("xy_used"))
        yacc_zero, yacc_clear = sem("yacc_zero"), sem("yacc_clear")
        stats_done = sem("stats_done")
        yT_ps, x_added, pool_turn, act_turn, xcur_ready = (
            sem("yT_ps"), sem("x_added"), sem("pool_turn"), sem("act_turn"), sem("xcur_ready"))

        class Steps:
            def __init__(self, eng, s):
                self.eng, self.sem, self.base, self.n = eng, s, 0, 0

            def link(self, ins):
                self.n += 1
                ins.then_inc(self.sem, 1)
                self.eng.wait_ge(self.sem, self.base + self.n)

            def enter(self, i, each):
                self.outer, self.each = self.base + self.n, each
                self.base, self.n = i * each + self.outer, 0

            def leave(self, times):
                assert self.n == self.each, (self.n, self.each)
                self.base, self.n = self.outer + times * self.each, 0

        def experts(name, index, route, w_dram, count, unroll, chunks, gated, func):
            f = Experts()
            f.name, f.index, f.route, f.w, f.E, f.U, f.nf, f.gated, f.func = (
                name, index, route, w_dram, count, unroll, chunks, gated, func)
            f.wc = chunks * P * (3 if gated else 2)
            f.iters = count // unroll
            f.NS = unroll * NB
            f.NK = f.NS * chunks
            f.w_in = [sem(f"{name}_w_in{s}") for s in range(unroll)]
            f.cb_in = [sem(f"{name}_cb_in{s}") for s in range(unroll)] if route is not None else None
            f.split = sem(f"{name}_split")
            f.wsplit_hi = sem(f"{name}_wsplit_hi")
            f.g_ready = sem(f"{name}_g_ready")
            f.g_used = sem(f"{name}_g_used")
            f.u_ready = sem(f"{name}_u_ready")
            f.hh_done = sem(f"{name}_hh_done")
            f.hf_done = sem(f"{name}_hf_done")
            f.h_ready = sem(f"{name}_h_ready")
            f.h_used = sem(f"{name}_h_used")
            f.y_used = sem(f"{name}_y_used")
            return f

        LAG = 3
        H_BANKS = (2, 3, 6, 7)

        def weights_free(f):
            return 7 if f.index == 7 else f.index - 1

        def y_banks(f):
            return 2 if f.gated else 4

        def h_bank(f, k):
            return bank(H_BANKS[k % 4] if f.gated else k % 4)

        phases = []
        phases.append(("attn", 0))
        phases.append(("ffn", experts("f0", 1, 0, f0, NE, 2, 2, False, ACT.Gelu)))
        phases.append(("attn", 1))
        phases.append(("ffn", experts("f1", 3, None, f1, NE, 2, 4, True, ACT.Silu)))
        phases.append(("attn", 2))
        phases.append(("ffn", experts("f2", 5, 1, f2, NE + 1, 3, 4, False, ACT.Silu)))
        phases.append(("wide", None))
        phases.append(("ffn", experts("f3", 7, 2, f3, NE, 2, 4, True, ACT.Silu)))
        phases = phases[:PHASES]
        FF = {2: 0, 4: 1, 6: 2, 7: 3, 8: 4}

        block = stack.enter_context(nc.Block())

        def bcast(ap, n, at):
            ap = ap.unsqueeze(at)
            return ap.broadcast_to([n if d == at else size for d, size in enumerate(ap.shape)])

        @block.sync
        def _(sp):
            sp.dma_start(ctxT[:], ctx_t).then_inc(ctx_loaded, 16)
            sp.dma_start(aw[:], attn_w).then_inc(ctx_loaded, 16)
            sp.dma_start(pcols[:], cols).then_inc(small_loaded, 16)
            sp.dma_start(prows[:, 0:2, :], bcast(rows[0:2, :], P, 0)).then_inc(small_loaded, 16)
            sp.dma_start(worow[:], rows[2:3, :]).then_inc(small_loaded, 16)
            sp.dma_start(m0u, mask0.rearrange("b o (t p) k -> p (b o t) k", p=P)).then_inc(mask_loaded, 16)
            sp.dma_start(m1i, bcast(mask1, P, 0)).then_inc(mask_loaded, 16)
            sp.dma_start(m2u, mask2.rearrange("b o (t p) k -> p (b o t) k", p=P)).then_inc(mask_loaded, 16)
            sp.dma_start(x[:], x_in.rearrange("b (t p) d -> p (b t) d", p=P)).then_inc(x_loaded, 16)
            sp.dma_start(gw[:], gates.rearrange("p (n e) -> p n e", n=3)).then_inc(late_loaded, 16)
            sp.dma_start(xc[:], xcols).then_inc(late_loaded, 16)
            sp.dma_start(crow, ctx_rows.rearrange("b k d -> k b d")).then_inc(late_loaded, 16)

            for kind, f in phases:
                if kind == "wide":
                    sp.wait_ge(x_done, 6)
                    with sp.Fori(0, LH // HB) as i:
                        for e in range(HB):
                            s = e % 2
                            sp.wait_ge(x_split, i * HB + (e + 1))
                            sp.dma_start(wraw[:, s * 512:(s + 1) * 512],
                                         xw[ds(i * HB + e, 1), :, :].rearrange("e p n -> p (e n)")
                                         ).then_inc(xw_in[s], 16)
                if kind != "ffn":
                    continue
                routed = f.route is not None
                if routed:
                    sp.wait_ge(consts, 1)
                    sp.dma_start(comb_dram[f.route][NE, :].rearrange("(a n) -> a n", n=P), one_rows[:]
                                 ).then_inc(comb_stored, 16)
                if f.index > 1:
                    sp.wait_ge(x_done, weights_free(f))
                with sp.Fori(0, f.iters) as i:
                    for s in range(f.U):
                        sp.wait_ge(f.split, i * f.U + (s + 1))
                        sp.dma_start(wraw[:, s * f.wc:(s + 1) * f.wc],
                                     f.w[ds(i * f.U + s, 1), :, :].rearrange("e p n -> p (e n)")
                                     ).then_inc(f.w_in[s], 16)
                    if routed:
                        sp.wait_ge(comb_stored, 32 * (f.route + 1))
                    for s in range(f.U if routed else 0):
                        sp.wait_ge(f.y_used, i * f.NS + (s + 1) * NB)
                        sp.dma_start(combs[s],
                                     comb_dram[f.route][ds(i * f.U + s, 1), :].broadcast_to([P, NT * P])).then_inc(f.cb_in[s], 16)
            sp.wait_ge(x_done, len(phases))
            sp.dma_start(out.rearrange("b (t p) d -> p (b t) d", p=P), x[:]).then_inc(out_stored, 16)
            sp.wait_ge(out_stored, 16)

        @block.gpsimd
        def _(pool):
            st = Steps(pool, pool_step)
            g = nc.gpsimd
            g.memset(ident[:], 0.0)
            g.memset(identb[:], 0.0)
            g.memset(media[:].bitcast(f32), 0.0)
            g.memset(ones_row[:], 1.0)
            g.memset(one_rows[:], 1.0)
            g.memset(hmask[:], 1.0)
            g.memset(cmask[:], 1.0)
            g.memset(spreadp[:], 0.0)
            g.memset(prows[:, 2, :], 0.0)
            st.link(g.memset(tri[:], 1.0))
            for m in (ident, identb):
                g.affine_select(out=m[:], in_=m[:], compare_op=ALU.not_equal, fill=1.0, base=0,
                                pattern=[[-1, P]], channel_multiplier=1)
            st.link(g.affine_select(out=hmask[:], in_=hmask[:], compare_op=ALU.is_ge, fill=0.0, base=0,
                                    pattern=[[-HD, H]], channel_multiplier=1))
            g.affine_select(out=hmask[:], in_=hmask[:], compare_op=ALU.is_ge, fill=0.0, base=HD - 1,
                            pattern=[[HD, H]], channel_multiplier=-1)
            for j in range(NCH):
                g.affine_select(out=cmask[:, j], in_=cmask[:, j], compare_op=ALU.is_ge, fill=0.0,
                                base=CH * j, pattern=[[0, NG], [-KC, HG]], channel_multiplier=1)
            st.link(g.affine_select(out=spread, in_=spread, compare_op=ALU.not_equal, fill=1.0, base=0,
                                    pattern=[[0, HG], [-1, KC]], channel_multiplier=1))
            for j in range(NCH):
                g.affine_select(out=cmask[:, j], in_=cmask[:, j], compare_op=ALU.is_ge, fill=0.0,
                                base=KC - 1 - CH * j, pattern=[[0, NG], [KC, HG]], channel_multiplier=-1)
            st.link(g.affine_select(out=tri[:], in_=tri[:], compare_op=ALU.is_ge, fill=0.0, base=-1,
                                    pattern=[[1, NE], [-1, NE]], channel_multiplier=0))
            for s in range(2):
                last = g.tensor_copy(vx[s][:, :, :, HD:VC],
                                     cmask[:].rearrange("r j g h -> r j (g h)").unsqueeze(3))
            last.then_inc(consts, 1)

            def clear_yacc(n):
                pool.wait_ge(xT_ps, NB * (n + 1))
                pool.sem_inc(pool_turn, 1)
                g.memset(yacc, 0.0).then_inc(yacc_zero, 1)

            for n, (kind, f) in enumerate(phases):
                if kind == "attn":
                    l = f
                    pool.wait_ge(kl_done, l + 1)
                    with pool.Fori(0, 2) as i:
                        for s in range(2):
                            it = i + 2 * l
                            pool.wait_ge(s_ready, it * 32 + (CREDIT + 16 * (s + 1) - 32))
                            for src, dst in ((kh, kbh), (kl, kbl)):
                                ins = g.tensor_tensor(
                                    out=dst[s].rearrange("p (h k) -> p h k", h=H),
                                    in0=bcast(src[:, l, ds(i * 2 * KC + s * KC, KC)].bitcast(f32), H, 1),
                                    in1=bcast(hmask[:], KC, 2), op=ALU.mult)
                            ins.then_inc(kb_ready, 1)
                elif kind == "wide":
                    pool.sem_inc(x_split, 2)
                    pool.wait_ge(x_done, 6)
                    clear_yacc(n)
                    pool.wait_ge(yacc_zero, FF[n + 1] + 1)
                    pool.sem_inc(pool_turn, 1)
                    g.tensor_scalar(yacc, yacc, xc[:, 3 * LH:3 * LH + 1], 1.0, ALU.add, ALU.mult).then_inc(yacc_clear, 1)
                    with pool.Fori(0, LH // HB) as i:
                        def split(e):
                            s = e % 2
                            raw, w = wraw[:, s * 512:(s + 1) * 512], slice(s * 512, (s + 1) * 512)
                            pool.wait_ge(xw_in[s], i * 8 * HB + 16 * (e // 2 + 1))
                            pool.wait_ge(xy_ready, i * UB + NB * (e + 1))
                            pool.sem_inc(pool_turn, 1)
                            g.tensor_scalar(raw[:, 0:P], raw[:, 0:P], LD ** -0.5, 1.0, ALU.mult, ALU.mult
                                            ).then_inc(x_scaled, 1)
                            pool.wait_ge(x_scaled, i * HB + (e + 1))
                            pool.sem_inc(pool_turn, 1)
                            g.tensor_scalar(wh[:, w], raw, 1.0, 1.0, ALU.mult, ALU.mult).then_inc(x_split_hi, 1)
                            pool.wait_ge(x_split_hi, i * HB + (e + 1))
                            g.tensor_tensor(out=wl[:, w], in0=raw, in1=wh[:, w].bitcast(f32),
                                            op=ALU.subtract).then_inc(x_split, 1)

                        for e in range(HB):
                            split(e)
                else:
                    for s in range(f.U):
                        pool.sem_inc(f.split, 1)
                    if f.index > 1:
                        pool.wait_ge(x_done, weights_free(f))
                    clear_yacc(n)
                    with pool.Fori(0, f.iters) as i:
                        for s in range(f.U):
                            sl = slice(s * f.wc, (s + 1) * f.wc)
                            pool.wait_ge(f.w_in[s], i * 16 + 16)
                            pool.wait_ge(f.h_used, i * f.NK + (s + 1) * NB * f.nf)
                            pool.sem_inc(pool_turn, 1)
                            g.tensor_scalar(wh[:, sl], wraw[:, sl], 1.0, 1.0, ALU.mult, ALU.mult).then_inc(f.wsplit_hi, 1)
                            pool.wait_ge(f.wsplit_hi, i * f.U + (s + 1))
                            g.tensor_tensor(out=wl[:, sl], in0=wraw[:, sl], in1=wh[:, sl].bitcast(f32),
                                            op=ALU.subtract).then_inc(f.split, 1)

        @block.scalar
        def _(act):
            a = nc.scalar
            for l in range(3):
                act.wait_ge(k_free, l + 1)
                a.activation(kh[:, l, :], kf, ACT.Copy).then_inc(kh_done, 1)
            act.wait_ge(ctx_loaded, 32)
            for l, c in enumerate((0, 4, 7)):
                ins = a.activation(wqh[:, l * P:(l + 1) * P], aw[:, c * P:(c + 1) * P], ACT.Copy)
            ins.then_inc(wq_hi, 1)

            for n, (kind, f) in enumerate(phases):
                for b in range(NB):
                    if kind == "wide":
                        act.wait_ge(xg_ready, b + 1)
                    else:
                        act.wait_ge(xT_ps, NB * n + b + 1)
                    a.activation(xh[:, b * 512:(b + 1) * 512], xg[b % 2] if kind == "wide" else bank(b), ACT.Copy
                                 ).then_inc(xh_done, 1)
                if kind == "wide":
                    with act.Fori(0, LH // HB) as i:
                        def high(u, part):
                            s, w = u % 2, i * UB + u
                            e = u // NB
                            act.wait_ge(pj_ps, w * 4 + (part + 1))
                            if part == 0:
                                ins = a.activation(qh[s][:], bank(0), ACT.Identity, bias=xcur[:, 0, e:e + 1])
                            elif part == 1:
                                ins = a.activation(kxh[s][:, 0:S], bank(0), ACT.Identity,
                                                   bias=xcur[:, 1, e:e + 1])
                            elif part == 2:
                                a.activation(kxh[s][:, S:S + KP], bank(0, KP), ACT.Identity,
                                             bias=xcur[:, 1, e:e + 1])
                                ins = a.activation(vxa[0:KC, s, 0, 512:640], bank(0)[0:KC, 128:256], ACT.Copy)
                            else:
                                ins = a.activation(vxa[:, s, 0, 0:512], bank(0), ACT.Copy)
                            ins.then_inc(pj_hi, 1)

                        def softmax(m):
                            act.wait_ge(xs_max, i * 4 * UB + (m + 1))
                            if m >= XS:
                                act.wait_ge(xt_ready, i * 4 * UB + (m - XS + 1))
                            z = slice(m % XS, m % XS + 1)
                            a.activation(xprob[m % XS], bank(2 + 2 * (m % 2), KEYS), ACT.Exp,
                                         bias=xnm[:, z], accum_out=xsum[:, z]).then_inc(x_exp, 1)

                        def turned(m):
                            u, qt = m // 4, m % 4
                            act.wait_ge(xt_ready, i * 4 * UB + (m + 1))
                            if u >= 2:
                                act.wait_ge(xo_ready, i * UB + (u - 1))
                            a.activation(xp4[u % 2][0].rearrange("p (j q) -> p j q", j=4)[:, :, qt * P:(qt + 1) * P],
                                         bank(6).rearrange("p (j q) -> p j q", j=4), ACT.Copy)
                            a.activation(xp5[u % 2][0][0:KC, qt * P:(qt + 1) * P], bank(7)[0:KC, 0:P], ACT.Copy
                                         ).then_inc(xt_hi, 1)

                        def attended(u):
                            act.wait_ge(xo_ready, i * UB + (u + 1))
                            a.activation(oxh, bank(1), ACT.Identity,
                                         bias=xcur[:, 2, u // NB:u // NB + 1]).then_inc(xo_hi, 1)

                        act.sem_inc(act_turn, 1)
                        a.activation(xcur[:], xc[:, 0:3 * LH].rearrange("p (c h) -> p c h", h=LH)[:, :, ds(i * HB, HB)],
                                     ACT.Copy).then_inc(xcur_ready, 1)
                        act.wait_ge(xcur_ready, i + 1)
                        for part in range(4):
                            high(0, part)
                        for u in range(UB + 1):
                            for qt in range(4):
                                m = 4 * u + qt
                                if 2 <= m < 4 * UB + 2:
                                    turned(m - 2)
                                if m < 4 * UB:
                                    softmax(m)
                                if u < UB - 1:
                                    high(u + 1, qt)
                                if u and qt == 3:
                                    attended(u - 1)
                        act.wait_ge(xy_used, i * UB + UB)
                if kind == "attn":
                    l, lo = f, (0 if f == 0 else 1)
                    with act.Fori(0, 2) as i:
                        it, io = i + 2 * l, i + 2 * lo

                        def prep(s):
                            act.wait_ge(q_evac, it * 2 + (s + 1))
                            a.activation(qh[s][:], qf, ACT.Copy).then_inc(qh_done, 1)

                        def copy_pT(n):
                            act.wait_ge(pt_ready, it * 32 + (n + 1))
                            if n >= 2:
                                act.wait_ge(pv_done, it * 32 + (n - 1))
                            a.activation(pT[n % 2][:], bank(2 + n % 2, NCH * P)[0:CH, :], ACT.Copy
                                         ).then_inc(pt_done, 1)

                        def copy_oT(t):
                            act.wait_ge(ont_ready, io * 8 + (t + 1))
                            a.activation(oT, bank(6)[:, 0:P], ACT.Copy).then_inc(ot_done, 1)

                        prep(0)
                        for t in range(8 + 2):
                            if t == 2:
                                prep(1)
                            for gr in range(NG):
                                if 1 <= t < 9:
                                    copy_pT(4 * (t - 1) + gr)
                                if gr == 1 and t >= 2 and l != 1:
                                    copy_oT(t - 2)
                            if t < 8:
                                act.wait_ge(s_used, it * 32 + (CREDIT + 4 * t + 4))
                                a.activation(probs[t % 2][:, :, 0:GW], shifted[t % 2][:], ACT.Exp
                                             ).then_inc(p_ready, 1)
                        act.wait_ge(x_upd, it * 8 + 8)
                if kind == "ffn":
                    if f.route is not None:
                        act.wait_ge(lsub_ready, f.route + 1)
                        a.activation(lexp[:], lsub[:], ACT.Exp).then_inc(lexp_ready, 1)
                        for b in range(NB):
                            act.wait_ge(combT_ps, NB * f.route + b + 1)
                            a.activation(combT[:, b * 512:(b + 1) * 512], bank(4 + b)[0:NE, :], ACT.Copy
                                         ).then_inc(combT_done, 1)
                        act.wait_ge(combT_done, NB * (f.route + 1))
                        a.dma_start(comb_dram[f.route][0:NE, :], combT).then_inc(comb_stored, 16)
                        if f.route == 0:
                            act.wait_ge(med_f, 1)
                            a.activation(mh.rearrange("p (b k) -> p b k", b=B)[:, :, 0:KC],
                                         med_full.rearrange("p (b k) -> p b k", b=B), ACT.Copy).then_inc(med_hi, 1)
                    if f.gated:
                        act.sem_inc(f.g_used, 2)
                    with act.Fori(0, f.iters) as i:
                        def func(k):
                            act.wait_ge(f.g_ready, i * f.NK + (k + 1))
                            if f.gated:
                                act.wait_ge(f.hf_done, i * f.NK + (k + 1))
                                ins = a.activation(act_out[k % 2][:], bank(k % 2), f.func)
                            else:
                                ins = a.activation(bank(k % 4), bank(k % 4), f.func)
                            ins.then_inc(f.g_used, 1)

                        def high(k):
                            if f.gated:
                                act.wait_ge(f.hf_done, i * f.NK + (k + 3))
                            else:
                                act.wait_ge(f.g_used, i * f.NK + (k + 1))
                            act.wait_ge(f.h_used, i * f.NK + (f.NK + k - 3))
                            a.activation(hh[k % 4], h_bank(f, k), ACT.Copy).then_inc(f.hh_done, 1)

                        for k in range(f.NK + 1):
                            if k < f.NK:
                                func(k)
                            if k >= 1:
                                high(k - 1)

        @block.vector
        def _(dve):
            v = nc.vector
            st = Steps(dve, dve_step)
            dve.wait_ge(ctx_loaded, 32)
            dve.wait_ge(small_loaded, 48)
            dve.wait_ge(consts, 1)
            for l, c in enumerate((0, 2, None)):
                dve.wait_ge(k_ps, l + 1)
                if l:
                    dve.wait_ge(kl_done, l)
                if c is None:
                    ins = v.tensor_scalar(kf, bank(0, B * KC), HD ** -0.5, None, ALU.mult)
                else:
                    ins = v.tensor_scalar(kf, bank(0, B * KC), pcols[:, c + 1:c + 2], HD ** -0.5,
                                          ALU.add, ALU.mult)
                ins.then_inc(k_free, 1)
                dve.wait_ge(v_ps, l + 1)
                v.tensor_tensor(vall[:, l, :].rearrange("k (b d) -> k b d", b=B),
                                bank(1)[0:KC, :].rearrange("k (b d) -> k b d", b=B),
                                bcast(prows[0:KC, l, :], B, 1), ALU.add).then_inc(v_done, 1)
                dve.wait_ge(kh_done, l + 1)
                v.tensor_tensor(kl[:, l, :], kf, kh[:, l, :].bitcast(f32), ALU.subtract).then_inc(kl_done, 1)
            dve.wait_ge(wq_hi, 1)
            for l, c in enumerate((0, 4, 7)):
                ins = v.tensor_tensor(wql[:, l * P:(l + 1) * P], aw[:, c * P:(c + 1) * P],
                                      wqh[:, l * P:(l + 1) * P].bitcast(f32), ALU.subtract)
            ins.then_inc(wq_lo, 1)
            dve.wait_ge(mask_loaded, 48)
            v.tensor_scalar(maskneg[:, 0], m0u, NEG, None, ALU.mult)
            st.link(v.tensor_scalar(m1f, m1i, 0.0, None, ALU.is_gt))
            v.tensor_reduce(seen[:], m1f, AX.X, ALU.min)
            for b in range(B):
                v.tensor_scalar(maskneg[:, 1, b * TB:(b + 1) * TB], bcast(m1f[:, b], TB, 1), NEG, None, ALU.mult)
            for b in range(B):
                ins = v.tensor_scalar(maskneg[:, 2, b * TB:(b + 1) * TB], m2u, -NEG, NEG, ALU.mult, ALU.add)
            st.link(ins)
            st.link(v.tensor_scalar(seen[:], seen[:], -1.0, 1.0, ALU.mult, ALU.add))
            st.link(v.reciprocal(rden[:, 0:B], seen[:]))
            v.tensor_tensor(seen[:], seen[:], rden[:, 0:B], ALU.mult).then_inc(mask_done, 1)
            dve.wait_ge(late_loaded, 48)
            st.link(v.tensor_scalar(gwg[:], gw[:, 0, :], pcols[:, 4:5], None, ALU.mult))
            v.tensor_copy(gh[:, 0, :], gwg[:])
            st.link(v.tensor_copy(gh[:, 1:3, :], gw[:, 1:3, :]))
            v.tensor_tensor(gl[:, 0, :], gwg[:], gh[:, 0, :].bitcast(f32), ALU.subtract)
            st.link(v.tensor_tensor(gl[:, 1:3, :], gw[:, 1:3, :], gh[:, 1:3, :].bitcast(f32), ALU.subtract))
            st.link(v.memset(betaB[:], 1.0))
            v.tensor_scalar(betaB[:], betaB[:], pcols[:, 5:6], None, ALU.mult).then_inc(gate_done, 1)

            def rsqrt(dst, var, scale=None, rows=slice(0, P)):
                if scale is not None:
                    st.link(v.tensor_tensor(vpe[rows, :], var, scale, ALU.mult))
                    st.link(v.tensor_tensor(vpe[rows, :], vpe[rows, :], scale, ALU.mult))
                    var = vpe[rows, :]
                st.link(v.tensor_scalar(vpe[rows, :], var, EPS, None, ALU.add))
                v.tensor_scalar(nhv[rows, :], vpe[rows, :], -0.5, None, ALU.mult)
                st.link(v.tensor_scalar(seed[rows, :], vpe[rows, :].bitcast(i32), 1, None, ALU.arith_shift_right))
                st.link(v.tensor_scalar(dst.bitcast(i32), seed[rows, :], -1.0, 1597463007.0, ALU.mult, ALU.add))
                for _ in range(3):
                    st.link(v.tensor_tensor(rtmp[rows, :], dst, dst, ALU.mult))
                    st.link(v.tensor_tensor(rtmp[rows, :], rtmp[rows, :], nhv[rows, :], ALU.mult))
                    st.link(v.scalar_tensor_tensor(dst, rtmp[rows, :], 1.5, dst, ALU.add, ALU.mult))

            def block_stats(b, added):
                dve.wait_ge(x_added, added)
                for t in range(TB):
                    v.bn_stats(stats[:, b * TB + t, :], x[:, b * TB + t, :]).then_inc(stats_done, 1)

            def back_to_x(nth, banks):
                for b in range(NB):
                    dve.wait_ge(yT_ps, NB * nth + b + 1)
                    xb = x[:, b * TB:(b + 1) * TB, :]
                    v.tensor_tensor(xb, xb, bank(banks[b]).rearrange("p (t d) -> p t d", d=D), ALU.add
                                    ).then_inc(x_added, 1)
                    if b:
                        block_stats(b - 1, NB * nth + b)
                block_stats(NB - 1, NB * (nth + 1))
                dve.sem_inc(x_done, 1)

            def normalise_context():
                KB = slice(0, KC)
                for b in range(B):
                    ins = v.bn_stats(stats[KB, b, :], crow[:, b, :])
                st.link(ins)
                st.link(v.memset(mv[:], 1.0))
                for b in range(B):
                    ins = v.bn_aggr(mv[KB, b, :], stats[KB, b, :])
                st.link(ins)
                rsqrt(rstd[KB, :], mv[KB, :, 1], rows=KB)
                for b in range(B):
                    ins = v.tensor_scalar(crow[:, b, :], crow[:, b, :], mv[KB, b, 0:1], rstd[KB, b:b + 1],
                                          ALU.subtract, ALU.mult)
                ins.then_inc(med_ready, 1)
                st.link(v.tensor_scalar(xc[:, 0:LH], xc[:, 0:LH], LD ** -0.5, None, ALU.mult))
                dve.wait_ge(med_ps, 1)
                v.tensor_scalar(med_full, bank(2, B * KC), xc[:, 3 * LH + 1:3 * LH + 2],
                                xc[:, 3 * LH + 2:3 * LH + 3], ALU.mult, ALU.add).then_inc(med_f, 1)
                dve.wait_ge(med_hi, 1)
                mid = [m.rearrange("p (b k) -> p b k", b=B)[:, :, 0:KC] for m in (mh, ml)]
                v.tensor_tensor(mid[1], med_full.rearrange("p (b k) -> p b k", b=B), mid[0].bitcast(f32),
                                ALU.subtract).then_inc(med_lo, 1)
                dve.wait_ge(med_lo, 1)

            dve.wait_ge(x_loaded, 16)
            for n, (kind, f) in enumerate(phases):
                if n == 0:
                    for t in range(NT):
                        ins = v.bn_stats(stats[:, t, :], x[:, t, :])
                    st.link(ins)
                else:
                    dve.wait_ge(stats_done, NT * n)
                for t in range(NT):
                    ins = v.bn_aggr(mv[:, t, :], stats[:, t, :])
                st.link(ins)
                rsqrt(rstd[:], mv[:, :, 1])
                if kind == "wide":
                    rsqrt(rstd2[:], mv[:, :, 1], rstd[:])
                    st.link(v.tensor_tensor(rstd[:], rstd[:], rstd2[:], ALU.mult))
                def normalise(b):
                    for t in range(b * TB, (b + 1) * TB):
                        ins = v.tensor_scalar(xn[:, t, :], x[:, t, :], mv[:, t, 0:1], rstd[:, t:t + 1],
                                              ALU.subtract, ALU.mult)
                    ins.then_inc(xn_ready, 1)

                def x_low(b):
                    if kind == "wide":
                        dve.wait_ge(xT_ps, NB * n + b + 1)
                        if b >= 2:
                            dve.wait_ge(xl_done, NB * n + b - 1)
                        v.tensor_scalar(xg[b % 2], bank(b), xc[:, 3 * LH + 3:3 * LH + 4],
                                        xc[:, 3 * LH + 4:3 * LH + 5], ALU.mult, ALU.add).then_inc(xg_ready, 1)
                    dve.wait_ge(xh_done, NB * n + b + 1)
                    v.tensor_tensor(xl[:, b * 512:(b + 1) * 512], xg[b % 2] if kind == "wide" else bank(b),
                                    xh[:, b * 512:(b + 1) * 512].bitcast(f32), ALU.subtract).then_inc(xl_done, 1)

                normalise(0)
                normalise(1)
                for b in range(NB):
                    x_low(b)
                    if b + 2 < NB:
                        normalise(b + 2)
                if kind == "attn":
                    l, lo = f, (0 if f == 0 else 1)
                    if l == 0:
                        dve.sem_inc(s_used, CREDIT)
                    for s in range(2):
                        st.link(v.memset(probs[s][:, :, GW:GWP], 0.0))
                    per = 8 * (4 + 1) + (8 if l == 1 else 0)
                    with dve.Fori(0, 2) as i:
                        st.enter(i, per)
                        it, io = i + 2 * l, i + 2 * lo

                        def prep(s):
                            dve.wait_ge(q_ps, it * 2 + (s + 1))
                            if s:
                                dve.wait_ge(q_ready, it * 2 + s)
                            if l < 2:
                                ins = v.tensor_scalar(qf, bank(7), pcols[:, 2 * l:2 * l + 1], None, ALU.add)
                            else:
                                ins = v.tensor_copy(qf, bank(7))
                            ins.then_inc(q_evac, 1)
                            dve.wait_ge(qh_done, it * 2 + (s + 1))
                            v.tensor_tensor(ql[s][:], qf, qh[s][:].bitcast(f32), ALU.subtract).then_inc(q_ready, 1)
                            dve.wait_ge(vx_ps, it * 2 + (s + 1))
                            v.tensor_tensor(
                                vx[s][:, :, :, 0:HD].rearrange("r j h d -> r (j h) d"),
                                bank(7)[0:CH, 0:NCH * D].rearrange("r (n d) -> r n d", d=HD),
                                bcast(cmask[:].rearrange("r j g h -> r (j g h)"), HD, 2),
                                ALU.mult).then_inc(vx_ready, 1)

                        def shift(n):
                            dve.wait_ge(s_ready, it * 32 + (CREDIT + n + 1))
                            s3 = bank(n % 2, GW).rearrange("p (h k) -> p h k", h=HG)
                            st.link(v.tensor_reduce(smax[:, n % 2, :], s3, AX.X, ALU.max))
                            v.tensor_tensor(shifted[(n // 4) % 2][:, n % 4, :].rearrange("p (h k) -> p h k", h=HG),
                                            s3, bcast(smax[:, n % 2, :], KC, 2), ALU.subtract).then_inc(s_used, 1)

                        def norm(t):
                            dve.wait_ge(pv_done, it * 32 + (4 * t + 4))
                            o3 = bank(4 + t % 2, H * VC).rearrange("p (h c) -> p h c", h=H)
                            st.link(v.reciprocal(rden[:], o3[:, :, HD:VC].rearrange("p h c -> p (h c)")))
                            if l == 1:
                                st.link(v.tensor_scalar(rden[:], rden[:], seen[:, ds(2 * i + (t // 4), 1)], None, ALU.mult))
                            if t >= 2 and l != 1:
                                dve.wait_ge(ont_ready, io * 8 + (t - 1))
                            ins = v.tensor_tensor(onorm[t % 2][:], o3[:, :, 0:HD], bcast(rden[:], HD, 2), ALU.mult)
                            ins.then_inc(o_used, 1)
                            if l == 1:
                                dve.wait_ge(o_used, it * 8 + (t + 1))
                                xt = x[:, ds(i * 8 + t, 1), :]
                                v.tensor_tensor(xt, xt, onorm[t % 2][:].rearrange("p h d -> p (h d)").unsqueeze(1),
                                                ALU.add).then_inc(x_upd, 1)

                        def tile_stats(t):
                            dve.wait_ge(x_upd, it * 8 + (t + 1))
                            v.bn_stats(stats[:, ds(i * 8 + t, 1), :].rearrange("p t c -> p (t c)"),
                                       x[:, ds(i * 8 + t, 1), :].rearrange("p t c -> p (t c)")).then_inc(stats_done, 1)

                        def update(t):
                            dve.wait_ge(out_ready, io * 8 + (t + 1))
                            xt = x[:, ds(i * 8 + t, 1), :]
                            v.tensor_tensor(xt, xt, bank(6)[:, P:2 * P].unsqueeze(1), ALU.add).then_inc(x_upd, 1)

                        prep(0)
                        for t in range(8 + (2 if l != 1 else 1)):
                            if t == 2:
                                prep(1)
                            if t < 8:
                                if t >= 2:
                                    dve.wait_ge(p_ready, it * 8 + (t - 1))
                                for gr in range(NG):
                                    shift(4 * t + gr)
                            if l == 1 and 2 <= t:
                                tile_stats(t - 2)
                            if 1 <= t < 9:
                                norm(t - 1)
                            if t >= 3 and l != 1:
                                tile_stats(t - 3)
                            if t >= 2 and l != 1:
                                update(t - 2)
                        tile_stats(7)
                    st.leave(2)
                    dve.sem_inc(x_done, 1)
                elif kind == "wide":
                    dve.wait_ge(yacc_clear, 1)
                    with dve.Fori(0, LH // HB) as i:
                        def part_low(u, part):
                            s, w = u % 2, i * UB + u
                            dve.wait_ge(pj_hi, w * 4 + (part + 1))
                            add, sub = ALU.add, ALU.subtract
                            if part == 0:
                                ins = v.scalar_tensor_tensor(ql[s][:], bank(0), xc[:, ds(i * HB + u // NB, 1)],
                                                             qh[s][:].bitcast(f32), add, sub)
                            elif part == 1:
                                ins = v.scalar_tensor_tensor(kxl[s][:, 0:S], bank(0),
                                                             xc[:, ds(i * HB + (u // NB + LH), 1)],
                                                             kxh[s][:, 0:S].bitcast(f32), add, sub)
                            elif part == 2:
                                v.scalar_tensor_tensor(kxl[s][:, S:S + KP], bank(0, KP),
                                                       xc[:, ds(i * HB + (u // NB + LH), 1)],
                                                       kxh[s][:, S:S + KP].bitcast(f32), add, sub)
                                ins = v.tensor_tensor(vxa[0:KC, s, 1, 512:640], bank(0)[0:KC, 128:256],
                                                      vxa[0:KC, s, 0, 512:640].bitcast(f32), sub)
                            else:
                                ins = v.tensor_tensor(vxa[:, s, 1, 0:512], bank(0),
                                                      vxa[:, s, 0, 0:512].bitcast(f32), sub)
                            ins.then_inc(pj_lo, 1)

                        def row_max(m):
                            dve.wait_ge(xs_ready, i * 4 * UB + (m + 1))
                            v.tensor_reduce(xnm[:, m % XS:m % XS + 1], bank(2 + 2 * (m % 2), KEYS), AX.X, ALU.max,
                                            negate=True).then_inc(xs_max, 1)

                        def inverse(m):
                            dve.wait_ge(x_exp, i * 4 * UB + (m + 1))
                            if m >= XS:
                                dve.wait_ge(xt_ready, i * 4 * UB + (m - XS + 1))
                            z = slice(m % XS, m % XS + 1)
                            v.reciprocal(xrd[:, z], xsum[:, z]).then_inc(x_rec, 1)
                            dve.wait_ge(x_rec, i * 4 * UB + (m + 1))
                            v.tensor_scalar(xdiag[m % XS], ident[:], xrd[:, z], None, ALU.mult).then_inc(x_norm, 1)

                        def turned_low(m):
                            u, qt = m // 4, m % 4
                            dve.wait_ge(xt_hi, i * 4 * UB + (m + 1))
                            hi, lo = [xp4[u % 2][p].rearrange("p (j q) -> p j q", j=4)[:, :, qt * P:(qt + 1) * P]
                                      for p in range(2)]
                            v.tensor_tensor(lo, bank(6).rearrange("p (j q) -> p j q", j=4), hi.bitcast(f32),
                                            ALU.subtract)
                            hi, lo = [xp5[u % 2][p][0:KC, qt * P:(qt + 1) * P] for p in range(2)]
                            v.tensor_tensor(lo, bank(7)[0:KC, 0:P], hi.bitcast(f32), ALU.subtract
                                            ).then_inc(xt_lo, 1)

                        def attended_low(u):
                            dve.wait_ge(xo_hi, i * UB + (u + 1))
                            v.scalar_tensor_tensor(oxl, bank(1), xc[:, ds(i * HB + (u // NB + 2 * LH), 1)],
                                                   oxh.bitcast(f32), ALU.add, ALU.subtract).then_inc(xo_lo, 1)

                        def add_out(u):
                            dve.wait_ge(xy_ready, i * UB + (8 + u + 1))
                            yb = yacc[:, (u % NB) * 512:(u % NB + 1) * 512]
                            if u:
                                dve.wait_ge(xy_used, i * UB + u)
                            v.tensor_tensor(yb, yb, bank(1), ALU.add).then_inc(xy_used, 1)

                        for part in range(4):
                            part_low(0, part)
                        for u in range(UB + 2):
                            for qt in range(4):
                                m = 4 * u + qt
                                if m < 4 * UB:
                                    row_max(m)
                                if 1 <= m < 4 * UB + 1:
                                    inverse(m - 1)
                                if 2 <= m < 4 * UB + 2:
                                    turned_low(m - 2)
                                if u < UB - 1:
                                    part_low(u + 1, qt)
                                if 1 <= u < UB + 1 and qt == 3:
                                    attended_low(u - 1)
                                if u >= 2 and qt == 0:
                                    add_out(u - 2)
                        dve.wait_ge(xy_used, i * UB + UB)
                    back_to_x(FF[7], (6, 7, 6, 7))
                else:
                    if f.route is not None:
                        if f.route == 0:
                            rsqrt(rstd2[:], mv[:, :, 1], rstd[:])
                        dve.wait_ge(lg_ps, f.route + 1)
                        lp, lq = [bank(4, NT * 2 * NE).rearrange("p (t e) -> p t e", e=2 * NE)[:, :, h * NE:(h + 1) * NE]
                                  for h in range(2)]
                        st.link(v.tensor_copy(logits[:], lp))
                        st.link(v.tensor_tensor(logits[:], logits[:], lq, ALU.add))
                        if f.route == 0:
                            v.tensor_copy(gbias[:], bank(4)[:, 256:256 + NE])
                            st.link(v.tensor_tensor(logits[:], logits[:], bcast(rstd2[:], NE, 2), ALU.mult))
                            st.link(v.tensor_tensor(logits[:], logits[:], bcast(gbias[:], NT, 1), ALU.add))
                        st.link(v.tensor_reduce(lmax[:], logits[:], AX.X, ALU.max))
                        v.tensor_tensor(lsub[:], logits[:], bcast(lmax[:], NE, 2), ALU.subtract).then_inc(lsub_ready, 1)
                        mine, other = bcast(logits[:], NE, 3), bcast(logits[:], NE, 2)
                        st.link(v.tensor_tensor(tied[:], other, mine, ALU.is_equal))
                        st.link(v.tensor_tensor(tied[:], tied[:], bcast(tri[:], NT, 1), ALU.mult))
                        st.link(v.tensor_tensor(above[:], other, mine, ALU.is_gt))
                        st.link(v.tensor_tensor(above[:], above[:], tied[:], ALU.add))
                        st.link(v.tensor_reduce(rank[:], above[:], AX.X, ALU.add))
                        st.link(v.tensor_scalar(rank[:], rank[:], 2.0, None, ALU.is_lt))
                        dve.wait_ge(lexp_ready, f.route + 1)
                        st.link(v.tensor_tensor(comb[:], lexp[:], rank[:], ALU.mult))
                        st.link(v.tensor_reduce(wsum[:], (lexp if f.route == 0 else comb)[:], AX.X, ALU.add))
                        st.link(v.reciprocal(wsum[:], wsum[:]))
                        v.tensor_tensor(comb[:], comb[:], bcast(wsum[:], NE, 2), ALU.mult).then_inc(comb_ready, 1)
                    if f.route == 0:
                        normalise_context()
                    if f.gated:
                        dve.sem_inc(f.hf_done, 2)
                    dve.sem_inc(f.h_ready, 4)
                    dve.sem_inc(f.y_used, f.NS)
                    dve.wait_ge(yacc_zero, FF[n + 1] + 1)
                    with dve.Fori(0, f.iters) as i:
                        st.enter(i, f.NS if f.route is not None else 0)

                        def low(k):
                            if f.gated:
                                dve.wait_ge(f.g_used, i * f.NK + (k + 3))
                                dve.wait_ge(f.u_ready, i * f.NK + (k + 1))
                                v.tensor_tensor(h_bank(f, k), act_out[k % 2][:], h_bank(f, k), ALU.mult
                                                ).then_inc(f.hf_done, 1)

                        def finish_low(k):
                            dve.wait_ge(f.hh_done, i * f.NK + (k + 1))
                            ins = v.tensor_tensor(hl[k % 4], h_bank(f, k), hh[k % 4].bitcast(f32), ALU.subtract)
                            ins.then_inc(f.h_ready, 1)

                        def result(s):
                            dve.wait_ge(f.h_used, i * f.NK + (f.NK + (s + 1) * f.nf))
                            if s:
                                dve.wait_ge(f.y_used, i * f.NS + (f.NS + s))
                            e, b = s // NB, s % NB
                            sl = slice(b * 512, (b + 1) * 512)
                            y = bank(4 + s % y_banks(f))
                            if f.route is not None:
                                if b == 0:
                                    dve.wait_ge(f.cb_in[e], i * 16 + 16)
                                st.link(v.tensor_tensor(y, y, combs[e][:, sl], ALU.mult))
                            v.tensor_tensor(yacc[:, sl], yacc[:, sl], y, ALU.add).then_inc(f.y_used, 1)

                        done = 0
                        for k in range(f.NK + 1):
                            if k < f.NK:
                                low(k)
                            if k >= 1:
                                finish_low(k - 1)
                            if k >= f.nf * (done + 1) + LAG:
                                result(done)
                                done += 1
                        while done < f.NS:
                            result(done)
                            done += 1
                        dve.wait_ge(f.y_used, i * f.NS + 2 * f.NS)
                    st.leave(f.iters)
                    back_to_x(FF[f.index + 1], (6, 7, 6, 7) if f.gated else (4, 5, 6, 7))

        @block.tensor
        def _(pe):
            mm = nc.tensor.matmul

            def mm3(dst, lh, ll, rh, rl, start=True, stop=True):
                mm(dst, ll, rh, start=start, stop=False)
                mm(dst, lh, rl, start=False, stop=False)
                return mm(dst, lh, rh, start=False, stop=stop)

            pe.wait_ge(ctx_loaded, 32)
            for l, (ck, cv) in enumerate(((1, 2), (5, 6), (8, 9))):
                if l:
                    pe.wait_ge(k_free, l)
                mm(bank(0, B * KC), aw[:, ck * P:(ck + 1) * P], ctxT[:], start=True, stop=True).then_inc(k_ps, 1)
                if l:
                    pe.wait_ge(v_done, l)
                for b in range(B):
                    ins = mm(bank(1)[0:KC, b * D:(b + 1) * D], ctxT[:, b * KC:(b + 1) * KC],
                             aw[:, cv * P:(cv + 1) * P], start=True, stop=True)
                ins.then_inc(v_ps, 1)
            pe.wait_ge(k_free, 3)
            pe.wait_ge(v_done, 3)
            pe.wait_ge(consts, 1)

            def yacc_back(nth, banks, ready):
                for b in range(NB):
                    ready(b)
                    if banks[b] in banks[:b]:
                        pe.wait_ge(x_added, NB * nth + b - 1)
                    for t in range(TB):
                        ins = nc.tensor.transpose(bank(banks[b])[:, t * P:(t + 1) * P],
                                                  yacc[:, (b * TB + t) * P:(b * TB + t + 1) * P], ident[:])
                    ins.then_inc(yT_ps, 1)

            for n, (kind, f) in enumerate(phases):
                for b in range(NB):
                    pe.wait_ge(xn_ready, NB * n + b + 1)
                    for t in range(TB):
                        ins = nc.tensor.transpose(bank(b)[:, t * P:(t + 1) * P], xn[:, b * TB + t, :], ident[:])
                    ins.then_inc(xT_ps, 1)
                if kind == "attn":
                    l, lo = f, (0 if f == 0 else 1)
                    if l == 0:
                        pe.sem_inc(s_ready, CREDIT)
                        pe.wait_ge(wq_lo, 1)
                        pe.wait_ge(mask_done, 1)
                    pe.wait_ge(xl_done, NB * (n + 1))
                    with pe.Fori(0, 2) as i:
                        it, io = i + 2 * l, i + 2 * lo

                        def prep(s):
                            if s:
                                pe.wait_ge(vx_ready, it * 2 + s)
                            cur = ds(i * 1024 + s * 512, 512)
                            w = slice(l * P, (l + 1) * P)
                            mm3(bank(7), wqh[:, w], wql[:, w], xh[:, cur], xl[:, cur]).then_inc(q_ps, 1)
                            pe.wait_ge(q_evac, it * 2 + (s + 1))
                            for j in range(NCH):
                                ins = mm(bank(7)[0:CH, j * D:(j + 1) * D], spreadp[:, j * CH:(j + 1) * CH],
                                         vall[:, l, ds(i * 2 * D + s * D, D)], start=True, stop=True)
                            ins.then_inc(vx_ps, 1)

                        def scores(n):
                            t, gr = n // 4, n % 4
                            s, tq = t // 4, t % 4
                            if tq == 0 and gr == 0:
                                pe.wait_ge(q_ready, it * 2 + (s + 1))
                                pe.wait_ge(kb_ready, it * 2 + (s + 1))
                            pe.wait_ge(s_used, it * 32 + (CREDIT + n - 1))
                            q = slice(tq * P, (tq + 1) * P)
                            w = slice(gr * GW, (gr + 1) * GW)
                            dst = bank(n % 2, GW)
                            mm3(dst, qh[s][:, q], ql[s][:, q], kbh[s][:, w], kbl[s][:, w], stop=False)
                            mm(dst.rearrange("p (h k) -> p h k", h=HG), identb[:],
                               maskneg[:, l, ds(i * 8 + t, 1), :].broadcast_to([P, HG, KC]),
                               start=False, stop=True).then_inc(s_ready, 1)

                        def transp(n):
                            t, gr = n // 4, n % 4
                            if gr == 0:
                                pe.wait_ge(p_ready, it * 8 + (t + 1))
                            if n >= 2:
                                pe.wait_ge(pt_done, it * 32 + (n - 1))
                            for j in range(NCH):
                                ins = nc.tensor.transpose(bank(2 + n % 2)[0:CH, j * P:(j + 1) * P],
                                                          probs[t % 2][:, gr, j * CH:(j + 1) * CH], ident[:])
                            ins.then_inc(pt_ready, 1)

                        def values(n):
                            t, gr = n // 4, n % 4
                            if t % 4 == 0 and gr == 0:
                                pe.wait_ge(vx_ready, it * 2 + (t // 4 + 1))
                            if gr == 0 and t >= 2:
                                pe.wait_ge(o_used, it * 8 + (t - 1))
                            pe.wait_ge(pt_done, it * 32 + (n + 1))
                            for j in range(NCH):
                                ins = mm(bank(4 + t % 2)[:, gr * HG * VC:(gr + 1) * HG * VC],
                                         pT[n % 2][:, j * P:(j + 1) * P],
                                         vx[t // 4][:, j, gr * HG:(gr + 1) * HG, :].rearrange("r h c -> r (h c)"),
                                         start=(j == 0), stop=(j == NCH - 1))
                            ins.then_inc(pv_done, 1)

                        def turn(t):
                            pe.wait_ge(o_used, it * 8 + (t + 1))
                            if t >= 1:
                                pe.wait_ge(x_upd, it * 8 + t)
                            nc.tensor.transpose(bank(6)[:, 0:P], onorm[t % 2][:].rearrange("p h d -> p (h d)"),
                                                ident[:]).then_inc(ont_ready, 1)

                        def project(t):
                            pe.wait_ge(ot_done, io * 8 + (t + 1))
                            wo = aw[:, (3 if l == 0 else 10) * P:(4 if l == 0 else 11) * P]
                            ins = mm(bank(6)[:, P:2 * P], oT, wo, start=True, stop=(l != 0))
                            if l == 0:
                                ins = mm(bank(6)[:, P:2 * P], ones_row[:], worow[:], start=False, stop=True)
                            ins.then_inc(out_ready, 1)

                        prep(0)
                        for t in range(8 + 2):
                            if t == 2:
                                prep(1)
                            for gr in range(NG):
                                if t < 8:
                                    scores(4 * t + gr)
                                if 1 <= t < 9:
                                    transp(4 * (t - 1) + gr)
                                    if gr:
                                        values(4 * (t - 1) + gr - 1)
                                if gr == 1 and t >= 2 and l != 1:
                                    turn(t - 2)
                            if 1 <= t < 9:
                                values(4 * (t - 1) + 3)
                            if t >= 2 and l != 1:
                                project(t - 2)
                        pe.wait_ge(x_upd, it * 8 + 8)
                elif kind == "wide":
                    pe.wait_ge(xl_done, NB * (n + 1))
                    pe.sem_inc(xy_ready, 8)
                    with pe.Fori(0, LH // HB) as i:
                        def wt(u, c):
                            o = (u // NB % 2) * 512 + c * P
                            return wh[:, o:o + P], wl[:, o:o + P]

                        def project(u, part):
                            s, b, w = u % 2, u % NB, i * UB + u
                            tk = slice(b * S, (b + 1) * S)
                            md = slice(b * KP, (b + 1) * KP)
                            if part == 0 and u % NB == 0:
                                pe.wait_ge(x_split, i * HB + (2 + u // NB + 1))
                            if part or u:
                                pe.wait_ge(pj_lo, w * 4 + part)
                            if part == 0:
                                ins = mm3(bank(0), *wt(u, 0), xh[:, tk], xl[:, tk])
                            elif part == 1:
                                ins = mm3(bank(0), *wt(u, 1), xh[:, tk], xl[:, tk])
                            elif part == 2:
                                mm3(bank(0, KP), *wt(u, 1), mh[:, md], ml[:, md])
                                mc = slice(b * KP, b * KP + KC)
                                ins = mm3(bank(0)[0:KC, 128:256], mh[:, mc], ml[:, mc], *wt(u, 2))
                            else:
                                for t in range(TB):
                                    tt = slice(b * S + t * P, b * S + (t + 1) * P)
                                    ins = mm3(bank(0)[:, t * P:(t + 1) * P], xh[:, tt], xl[:, tt], *wt(u, 2))
                            ins.then_inc(pj_ps, 1)

                        def scores(m):
                            u, qt = m // 4, m % 4
                            s = u % 2
                            if qt == 0:
                                pe.wait_ge(pj_lo, i * 4 * UB + (u + 1) * 4)
                            if m >= 2:
                                pe.wait_ge(x_exp, i * 4 * UB + (m - 1))
                            q = slice(qt * P, (qt + 1) * P)
                            for c, w in ((0, S), (1, KP)):
                                kk = slice(c * S, c * S + w)
                                ins = mm3(bank(2 + 2 * (m % 2) + c, w), qh[s][:, q], ql[s][:, q],
                                          kxh[s][:, kk], kxl[s][:, kk])
                            ins.then_inc(xs_ready, 1)

                        def turn(m):
                            pe.wait_ge(x_norm, i * 4 * UB + (m + 1))
                            if m:
                                pe.wait_ge(xt_lo, i * 4 * UB + m)
                            for j in range(4):
                                mm(bank(6)[:, j * P:(j + 1) * P], xprob[m % XS][:, j * P:(j + 1) * P], xdiag[m % XS],
                                   start=True, stop=True)
                            mm(bank(7)[0:KC, 0:P], xprob[m % XS][:, S:KEYS], xdiag[m % XS], start=True, stop=True
                               ).then_inc(xt_ready, 1)

                        def attend(u, chunks):
                            s = u % 2
                            if chunks[0] == 4:
                                pe.wait_ge(xt_lo, i * 4 * UB + (4 * u + 4))
                                if u:
                                    pe.wait_ge(xy_used, i * UB + u)
                            for j in chunks:
                                vh, vl = [vxa[0:P if j < 4 else KC, s, p, j * P:(j + 1) * P] for p in range(2)]
                                ph, pl = [xp4[s][p][:, j * S:(j + 1) * S] if j < 4 else xp5[s][p][0:KC, :]
                                          for p in range(2)]
                                ins = mm3(bank(1), vh, vl, ph, pl, start=(j == 4), stop=(j == 3))
                            if chunks[-1] == 3:
                                ins.then_inc(xo_ready, 1)

                        def out_product(u):
                            pe.wait_ge(xo_lo, i * UB + (u + 1))
                            mm3(bank(1), *wt(u, 3), oxh, oxl).then_inc(xy_ready, 1)

                        for part in range(4):
                            project(0, part)
                        for u in range(UB + 2):
                            for qt in range(4):
                                m = 4 * u + qt
                                if m < 4 * UB:
                                    scores(m)
                                if 2 <= m < 4 * UB + 2:
                                    turn(m - 2)
                                if 1 <= u < UB + 1 and qt == 2:
                                    attend(u - 1, (4, 0))
                                if 1 <= u < UB + 1 and qt == 3:
                                    attend(u - 1, (1, 2, 3))
                                if u < UB - 1:
                                    project(u + 1, qt)
                                if u >= 2 and qt == 0:
                                    out_product(u - 2)
                        pe.wait_ge(xy_used, i * UB + UB)
                    yacc_back(FF[7], (6, 7, 6, 7), lambda b: None)
                else:
                    if f.route is None:
                        pe.wait_ge(xl_done, NB * (n + 1))
                    else:
                        pe.wait_ge(gate_done, 1)
                        r = f.route
                        for t in range(NT):
                            if t % TB == 0:
                                pe.wait_ge(xl_done, NB * n + t // TB + 1)
                            tk = slice(t * P, (t + 1) * P)
                            o = t * 2 * NE
                            mm(bank(4)[:, o:o + 2 * NE], xh[:, tk], ghl[:, r, :], start=True, stop=False)
                            ins = mm(bank(4)[:, o:o + NE], xl[:, tk], gh[:, r, :], start=False, stop=True)
                        if r == 0:
                            ins = mm(bank(4)[:, 256:256 + NE], betaB[:], gw[:, 0, :], start=True, stop=True)
                        ins.then_inc(lg_ps, 1)
                        pe.wait_ge(comb_ready, r + 1)
                        for b in range(NB):
                            for t in range(TB):
                                ins = nc.tensor.transpose(bank(4 + b)[0:NE, t * P:(t + 1) * P],
                                                          comb[:, b * TB + t, :], ident[:])
                            ins.then_inc(combT_ps, 1)
                        pe.wait_ge(combT_done, NB * (r + 1))
                        if r == 0:
                            pe.wait_ge(med_ready, 1)
                            for b in range(B):
                                ins = nc.tensor.transpose(bank(2)[:, b * KC:(b + 1) * KC], crow[:, b, :], ident[0:KC, 0:KC])
                            ins.then_inc(med_ps, 1)
                            pe.wait_ge(med_lo, 1)
                    pe.sem_inc(f.h_used, f.NK)
                    with pe.Fori(0, f.iters) as i:
                        def up(k):
                            s, c = k // f.nf, k % f.nf
                            e, b = s // NB, s % NB
                            if b == 0 and c == 0:
                                pe.wait_ge(f.split, i * f.U + (f.U + e + 1))
                            tk = slice(b * 512, (b + 1) * 512)
                            w = slice(e * f.wc + c * P, e * f.wc + (c + 1) * P)
                            if f.gated:
                                pe.wait_ge(f.g_used, i * f.NK + (k + 1))
                            else:
                                pe.wait_ge(f.h_ready, i * f.NK + (k + 1))
                            mm3(bank(k % 2 if f.gated else k % 4), wh[:, w], wl[:, w], xh[:, tk], xl[:, tk]).then_inc(f.g_ready, 1)
                            if f.gated:
                                w = slice(w.start + f.nf * P, w.stop + f.nf * P)
                                pe.wait_ge(f.h_ready, i * f.NK + (k + 1))
                                mm3(bank(H_BANKS[k % 4]), wh[:, w], wl[:, w], xh[:, tk], xl[:, tk]).then_inc(f.u_ready, 1)

                        def down(k):
                            s, c = k // f.nf, k % f.nf
                            e = s // NB
                            o = e * f.wc + (2 if f.gated else 1) * f.nf * P + c * P
                            if c == 0:
                                pe.wait_ge(f.y_used, i * f.NS + (f.NS + s - y_banks(f) + 1))
                            pe.wait_ge(f.h_ready, i * f.NK + (k + 5))
                            dst = bank(4 + s % y_banks(f))
                            mm(dst, wl[:, o:o + P], hh[k % 4], start=(c == 0), stop=False)
                            mm(dst, wh[:, o:o + P], hl[k % 4], start=False, stop=False)
                            ins = mm(dst, wh[:, o:o + P], hh[k % 4], start=False, stop=(c == f.nf - 1))
                            ins.then_inc(f.h_used, 1)

                        for k in range(f.NK + LAG):
                            if k < f.NK:
                                up(k)
                            if k >= LAG:
                                down(k - LAG)
                    yacc_back(FF[f.index + 1], (6, 7, 6, 7) if f.gated else (4, 5, 6, 7),
                              lambda b: pe.wait_ge(f.y_used, f.NS * (f.iters + 1) - (NB - 1 - b)))


_OUTS = [((4, 512, 128), 'float32')]


def kernel(**inputs):
    import numpy as _np
    import concourse.bacc as _bacc
    from concourse import mybir as _mybir
    from concourse.bass_utils import run_bass_kernel_spmd as _run

    g = {k: _np.asarray(v) for k, v in inputs.items()}

    def chunked(w):
        e, f, d = w.shape
        return w.reshape(e, f // 128, 128, d).transpose(0, 2, 1, 3).reshape(e, 128, -1)

    def heads(w):
        return w.reshape(128, 8, 128).transpose(1, 0, 2)

    cat = _np.concatenate
    packed = {
        "x": g["x"],
        "ctx_t": g["ctx_1024"].reshape(-1, 128).T,
        "ctx_rows": g["ctx_1024"],
        "mask0": g["mask_Bx1xSxS2_bk1"],
        "mask1": g["mask_BxS2_ik0"],
        "mask2": g["mask_1x1xSxS2_bk0"],
        "attn_w": cat([g["L0_xattn_Wq"], g["L0_xattn_Wk"], g["L0_xattn_Wv"], g["L0_xattn_Wo"],
                       g["L1_xattn_q_w"].T, g["L1_xattn_k_w"].T, g["L1_xattn_v_w"].T,
                       g["L2_xattn_Wq"].T, g["L2_xattn_Wk"].T, g["L2_xattn_Wv"].T, g["L2_xattn_Wo"].T], axis=1),
        "cols": _np.stack([g["L0_xattn_bq"], g["L0_xattn_bk"], g["L1_xattn_q_b"], g["L1_xattn_k_b"],
                           g["L0_ffn_ln_gamma"], g["L0_ffn_ln_beta"], g["L0_ffn_ln_gamma"],
                           g["L0_ffn_ln_beta"]], axis=1),
        "rows": _np.stack([g["L0_xattn_bv"], g["L1_xattn_v_b"], g["L0_xattn_bo"]]),
        "gates": cat([g["L0_ffn_gate_w"].T, g["L2_ffn_w_router"], g["L3_ffn_gate_w"]], axis=1),
        "f0": cat([g["L0_ffn_w1"].transpose(0, 2, 1), chunked(g["L0_ffn_w2"].transpose(0, 2, 1))], axis=2),
        "f1": cat([g["L1_ffn_Wg"], g["L1_ffn_Wu"], chunked(g["L1_ffn_Wd"])], axis=2),
        "f2": cat([cat([g["L2_ffn_w1_routed"], g["L2_ffn_w1_shared"][None]], axis=0),
                   chunked(cat([g["L2_ffn_w2_routed"], g["L2_ffn_w2_shared"][None]], axis=0))], axis=2),
        "f3": cat([g["L3_ffn_w1"], g["L3_ffn_w3"], chunked(g["L3_ffn_w2"])], axis=2),
        "xw": cat([heads(g["L3_xattn_Wq"]), heads(g["L3_xattn_Wkv"][:, :1024]), heads(g["L3_xattn_Wkv"][:, 1024:]),
                   g["L3_xattn_Wo"].reshape(8, 128, 128)], axis=2),
        "xcols": cat([g["L3_xattn_bq"].reshape(8, 128), g["L3_xattn_bkv"].reshape(16, 128),
                      g["L3_xattn_bo"][None], g["L3_xattn_gamma_media"][None], g["L3_xattn_beta_media"][None],
                      g["L3_xattn_gamma_lat"][None], g["L3_xattn_beta_lat"][None]], axis=0).T,
    }
    nc = _bacc.Bacc("TRN2", target_bir_lowering=False, num_devices=1)
    arrays, args = {}, []
    for name, a in packed.items():
        a = _np.ascontiguousarray(a)
        arrays[f"in_{name}_dram"] = a
        args.append(nc.dram_tensor(f"in_{name}_dram", a.shape, _mybir.dt.from_np(a.dtype), kind="ExternalInput").ap())
    for i, (shape, dtype) in enumerate(_OUTS):
        dt = _mybir.dt.from_np(_np.dtype(dtype))
        args.append(nc.dram_tensor(f"out_{i}_dram", shape, dt, kind="ExternalOutput").ap())
    build(nc, *args)
    r = _run(nc, [arrays], core_ids=[0])
    return r.results[0]["out_0_dram"]
```
